# Optimizing a Trainium2 kernel written in Bass

```python
import numpy as np
import jax
import jax.numpy as jnp

def _softmax(x, axis=-1):
    return jax.nn.softmax(x, axis=axis)

def _gelu(x):
    return jax.nn.gelu(x, approximate=True)

def _silu(x):
    return jax.nn.silu(x)

def _sigmoid(x):
    return jax.nn.sigmoid(x)

def _layernorm(x, axis=-1, eps=1e-05):
    m = jnp.mean(x, axis=axis, keepdims=True)
    v = jnp.var(x, axis=axis, keepdims=True)
    return (x - m) / jnp.sqrt(v + eps)

def _scatter_add(tgt, idx, src, axis=0):
    return tgt.at[idx].add(src)

def _segment_sum(src, seg, n):
    return jax.ops.segment_sum(src, seg, n)
kernel_name = 'mk_hybrid_d1_jaxref_r8_0824bc'

def setup_inputs(seed: int=0):
    np.random.seed(seed)
    _w = jnp.asarray

    def _L0_attn_a_setup():
        import jax, jax.numpy as jnp
        import numpy as np
        NEG_INF = -1e+30

        def rotary_pos_emb(x):
            B, T, H, D = x.shape
            exponents = (jnp.arange(0, D, 2)[:D // 2] // D).astype(jnp.float32)
            freqs = 1.0 / jnp.power(jnp.float32(1000.0), exponents)
            theta = jnp.arange(T, dtype=jnp.float32)[:, None] * freqs[None, :]
            cos = jnp.cos(theta)[None, :, None, :]
            sin = jnp.sin(theta)[None, :, None, :]
            xr = x.astype(jnp.float32).reshape(B, T, H, D // 2, 2)
            x0, x1 = (xr[..., 0], xr[..., 1])
            out = jnp.stack([x0 * cos - x1 * sin, x0 * sin + x1 * cos], axis=-1)
            return out.reshape(B, T, H, D).astype(x.dtype)

        def attention_fwd(x, wq, wk, wv, wo, n_heads=32):
            B, T, C = x.shape
            hd = C // n_heads
            xq = (x @ wq.T).reshape(B, T, n_heads, hd)
            xk = (x @ wk.T).reshape(B, T, n_heads, hd)
            xv = (x @ wv.T).reshape(B, T, n_heads, hd)
            xq = rotary_pos_emb(xq)
            xk = rotary_pos_emb(xk)
            scale = hd ** (-0.5)
            scores = jnp.einsum('bqhd,bkhd->bhqk', xq, xk) * scale
            causal = jnp.tril(jnp.ones((T, T), dtype=bool))
            scores = jnp.where(causal[None, None], scores, NEG_INF)
            probs = jax.nn.softmax(scores.astype(jnp.float32), axis=-1).astype(xq.dtype)
            out = jnp.einsum('bhqk,bkhd->bqhd', probs, xv).reshape(B, T, C)
            return out @ wo.T
        key = jax.random.key(seed)
        ks = jax.random.split(key, 5)
        B, T, C = (2, 256, 512)
        s = 0.02
        return {'x': jax.random.normal(ks[0], (B, T, C), jnp.float32), 'wq': jax.random.normal(ks[1], (C, C), jnp.float32) * s, 'wk': jax.random.normal(ks[2], (C, C), jnp.float32) * s, 'wv': jax.random.normal(ks[3], (C, C), jnp.float32) * s, 'wo': jax.random.normal(ks[4], (C, C), jnp.float32) * s}
    _L0_attn_a_in = _L0_attn_a_setup()

    def _L0_attn_b_setup():
        import jax, jax.numpy as jnp
        import numpy as np
        import math
        B, S, DM = (1, 256, 512)
        H, HKV, HD = (32, 8, 128)
        EPS = 1e-06
        NEG_INF = -1e+30

        def _alibi_slopes(n_heads: int) -> np.ndarray:
            start = 2 ** (-2 ** (-(math.log2(n_heads) - 3)))
            return np.array([start * start ** i for i in range(n_heads)], dtype=np.float32)

        def _rmsnorm(t, w):
            tf = t.astype(jnp.float32)
            inv = jax.lax.rsqrt(jnp.mean(tf * tf, axis=-1, keepdims=True) + EPS)
            return (tf * inv * w).astype(t.dtype)
        key = jax.random.key(seed)
        ks = jax.random.split(key, 5)
        std = 0.02
        return {'x': jax.random.normal(ks[0], (B, S, DM), dtype=jnp.float32), 'Wq': jax.random.normal(ks[1], (H * HD, DM), dtype=jnp.float32) * std, 'Wk': jax.random.normal(ks[2], (HKV * HD, DM), dtype=jnp.float32) * std, 'Wv': jax.random.normal(ks[3], (HKV * HD, DM), dtype=jnp.float32) * std, 'Wo': jax.random.normal(ks[4], (H * HD, DM), dtype=jnp.float32).T * (std / math.sqrt(2 * 32)), 'q_norm_w': jnp.ones((HD,), dtype=jnp.float32), 'k_norm_w': jnp.ones((HD,), dtype=jnp.float32)}
    _L0_attn_b_in = _L0_attn_b_setup()

    def _L0_ffn_setup():
        import jax, jax.numpy as jnp
        import numpy as np
        B, S, D, O, E, R = (2, 512, 512, 512, 8, 16)
        TOP_K = 2
        SCALING = 32.0 / 16.0
        key = jax.random.key(seed)
        k = jax.random.split(key, 6)
        x = jax.random.normal(k[0], (B, S, D), dtype=jnp.float32)
        W_base = jax.random.normal(k[1], (O, D), dtype=jnp.float32) * 0.02
        b_base = jax.random.normal(k[2], (O,), dtype=jnp.float32) * 0.02
        W_router = jax.random.normal(k[3], (E, D), dtype=jnp.float32) * 0.01
        lora_A = jax.random.normal(k[4], (E, R, D), dtype=jnp.float32) * (1.0 / np.sqrt(D))
        lora_B = jax.random.normal(k[5], (E, O, R), dtype=jnp.float32) * 0.02
        return {'x': x, 'W_base': W_base, 'b_base': b_base, 'W_router': W_router, 'lora_A': lora_A, 'lora_B': lora_B}
    _L0_ffn_in = _L0_ffn_setup()
    _d = {'L0_attn_a_x': _L0_attn_a_in['x'], 'L0_attn_a_wq': _L0_attn_a_in['wq'], 'L0_attn_a_wk': _L0_attn_a_in['wk'], 'L0_attn_a_wv': _L0_attn_a_in['wv'], 'L0_attn_a_wo': _L0_attn_a_in['wo'], 'L0_attn_b_Wq': _L0_attn_b_in['Wq'], 'L0_attn_b_Wk': _L0_attn_b_in['Wk'], 'L0_attn_b_Wv': _L0_attn_b_in['Wv'], 'L0_attn_b_Wo': _L0_attn_b_in['Wo'], 'L0_attn_b_q_norm_w': _L0_attn_b_in['q_norm_w'], 'L0_attn_b_k_norm_w': _L0_attn_b_in['k_norm_w'], 'L0_ffn_W_base': _L0_ffn_in['W_base'], 'L0_ffn_b_base': _L0_ffn_in['b_base'], 'L0_ffn_W_router': _L0_ffn_in['W_router'], 'L0_ffn_lora_A': _L0_ffn_in['lora_A'], 'L0_ffn_lora_B': _L0_ffn_in['lora_B']}
    _x0 = _d['L0_attn_a_x']
    _d['L0_attn_a_x'] = jax.random.normal(jax.random.fold_in(jax.random.key(seed), 1), (1, 1024, 512), dtype=_x0.dtype)
    del _x0
    return _d

def reference(L0_attn_a_x, L0_attn_a_wq, L0_attn_a_wk, L0_attn_a_wv, L0_attn_a_wo, L0_attn_b_Wq, L0_attn_b_Wk, L0_attn_b_Wv, L0_attn_b_Wo, L0_attn_b_q_norm_w, L0_attn_b_k_norm_w, L0_ffn_W_base, L0_ffn_b_base, L0_ffn_W_router, L0_ffn_lora_A, L0_ffn_lora_B):

    def _L0_attn_a_ref(x, wq, wk, wv, wo):
        import jax, jax.numpy as jnp
        import numpy as np
        NEG_INF = -1e+30

        def rotary_pos_emb(x):
            B, T, H, D = x.shape
            exponents = (jnp.arange(0, D, 2)[:D // 2] // D).astype(jnp.float32)
            freqs = 1.0 / jnp.power(jnp.float32(1000.0), exponents)
            theta = jnp.arange(T, dtype=jnp.float32)[:, None] * freqs[None, :]
            cos = jnp.cos(theta)[None, :, None, :]
            sin = jnp.sin(theta)[None, :, None, :]
            xr = x.astype(jnp.float32).reshape(B, T, H, D // 2, 2)
            x0, x1 = (xr[..., 0], xr[..., 1])
            out = jnp.stack([x0 * cos - x1 * sin, x0 * sin + x1 * cos], axis=-1)
            return out.reshape(B, T, H, D).astype(x.dtype)

        def attention_fwd(x, wq, wk, wv, wo, n_heads=32):
            B, T, C = x.shape
            hd = C // n_heads
            xq = (x @ wq.T).reshape(B, T, n_heads, hd)
            xk = (x @ wk.T).reshape(B, T, n_heads, hd)
            xv = (x @ wv.T).reshape(B, T, n_heads, hd)
            xq = rotary_pos_emb(xq)
            xk = rotary_pos_emb(xk)
            scale = hd ** (-0.5)
            scores = jnp.einsum('bqhd,bkhd->bhqk', xq, xk) * scale
            causal = jnp.tril(jnp.ones((T, T), dtype=bool))
            scores = jnp.where(causal[None, None], scores, NEG_INF)
            probs = jax.nn.softmax(scores.astype(jnp.float32), axis=-1).astype(xq.dtype)
            out = jnp.einsum('bhqk,bkhd->bqhd', probs, xv).reshape(B, T, C)
            return out @ wo.T
        return attention_fwd(x, wq, wk, wv, wo)

    def _L0_attn_b_ref(x, Wq, Wk, Wv, Wo, q_norm_w, k_norm_w):
        import jax, jax.numpy as jnp
        import numpy as np
        import math
        B, S, DM = (1, 256, 512)
        H, HKV, HD = (32, 8, 128)
        EPS = 1e-06
        NEG_INF = -1e+30

        def _alibi_slopes(n_heads: int) -> np.ndarray:
            start = 2 ** (-2 ** (-(math.log2(n_heads) - 3)))
            return np.array([start * start ** i for i in range(n_heads)], dtype=np.float32)

        def _rmsnorm(t, w):
            tf = t.astype(jnp.float32)
            inv = jax.lax.rsqrt(jnp.mean(tf * tf, axis=-1, keepdims=True) + EPS)
            return (tf * inv * w).astype(t.dtype)
        b, s, _ = x.shape
        G = H // HKV
        q = (x @ Wq.T).reshape(b, s, H, HD).transpose(0, 2, 1, 3)
        k = (x @ Wk.T).reshape(b, s, HKV, HD).transpose(0, 2, 1, 3)
        v = (x @ Wv.T).reshape(b, s, HKV, HD).transpose(0, 2, 1, 3)
        q = _rmsnorm(q, q_norm_w)
        k = _rmsnorm(k, k_norm_w)
        qg = q.reshape(b, HKV, G, s, HD)
        scores = jnp.einsum('bkgqd,bksd->bkgqs', qg, k) / math.sqrt(HD)
        slopes = jnp.asarray(_alibi_slopes(H)).reshape(HKV, G)
        pos = jnp.arange(s, dtype=jnp.float32)
        rel = pos[None, :] - pos[:, None]
        bias = jnp.where(rel > 0, NEG_INF, slopes[:, :, None, None] * rel)
        attn = jax.nn.softmax(scores + bias[None], axis=-1)
        out = jnp.einsum('bkgqs,bksd->bkgqd', attn, v)
        out = out.reshape(b, H, s, HD).transpose(0, 2, 1, 3).reshape(b, s, H * HD)
        return out @ Wo.T

    def _L0_ffn_ref(x, W_base, b_base, W_router, lora_A, lora_B):
        import jax, jax.numpy as jnp
        import numpy as np
        B, S, D, O, E, R = (2, 512, 512, 512, 8, 16)
        TOP_K = 2
        SCALING = 32.0 / 16.0
        d = x.shape[-1]
        n_experts = W_router.shape[0]
        xf = x.reshape(-1, d)
        logits = xf @ W_router.T
        probs = jax.nn.softmax(logits, axis=-1)
        topk_p, topk_i = jax.lax.top_k(probs, TOP_K)
        topk_p = topk_p / jnp.sum(topk_p, axis=-1, keepdims=True)
        w = jnp.sum(jax.nn.one_hot(topk_i, n_experts, dtype=xf.dtype) * topk_p[..., None], axis=1)
        h = jnp.einsum('td,erd->ter', xf, lora_A)
        lora_out = jnp.einsum('ter,eor,te->to', h, lora_B, w) * SCALING
        base = x @ W_base.T + b_base
        return base + lora_out.reshape(x.shape[:-1] + (W_base.shape[0],))
    x = L0_attn_a_x
    x = x + _L0_attn_a_ref(_layernorm(x, axis=-1), L0_attn_a_wq, L0_attn_a_wk, L0_attn_a_wv, L0_attn_a_wo)
    x = x + _L0_ffn_ref(_layernorm(x, axis=-1), L0_ffn_W_base, L0_ffn_b_base, L0_ffn_W_router, L0_ffn_lora_A, L0_ffn_lora_B)
    x = x + _L0_attn_b_ref(_layernorm(x, axis=-1), L0_attn_b_Wq, L0_attn_b_Wk, L0_attn_b_Wv, L0_attn_b_Wo, L0_attn_b_q_norm_w, L0_attn_b_k_norm_w)
    x = x + _L0_ffn_ref(_layernorm(x, axis=-1), L0_ffn_W_base, L0_ffn_b_base, L0_ffn_W_router, L0_ffn_lora_A, L0_ffn_lora_B)
    return x

_drawn_inputs = setup_inputs


def setup_inputs(seed=0):
    import zlib

    import numpy as np

    out = dict(_drawn_inputs(seed))
    spreads = {'L0_attn_b_q_norm_w': (1.0, 0.6), 'L0_attn_b_k_norm_w': (1.0, 0.6)}
    factors = {'L0_attn_a_wq': 7.298,
     'L0_attn_a_wk': 6.664,
     'L0_attn_a_wv': 2.704,
     'L0_attn_a_wo': 2.744,
     'L0_attn_b_Wq': 3.403,
     'L0_attn_b_Wk': 3.346}
    for name, (base, spread) in spreads.items():
        noise = np.random.default_rng([zlib.crc32(name.encode()), seed]).standard_normal(out[name].shape)
        drawn = base * np.exp(spread * noise) if base else spread * noise
        out[name] = jnp.asarray(drawn.astype(out[name].dtype))
    for name, factor in factors.items():
        out[name] = (out[name] * factor).astype(out[name].dtype)
    return out
```

```python
from contextlib import ExitStack

import numpy as np

import concourse.bass as bass
from concourse import mybir

F32 = mybir.dt.float32
F32R = mybir.dt.float32r
BF16 = mybir.dt.bfloat16
U32 = mybir.dt.uint32
ALU = mybir.AluOpType
ACT = mybir.ActivationFunctionType

P = 128
T = 1024
C = 512
NT = T // P
KC = C // P
W = 512
LN_EPS = 1e-5

HA, DA = 32, 16
GA = 4
NGA = HA // GA
SLOTS = 8

HB, KVB, DB = 32, 8, 128
GB = HB // KVB
RMS_EPS = 1e-6

NE, NR = 8, 16
ER = NE * NR
SCALING = 32.0 / 16.0

NEG = -1e30
SLIDE = T - P


def key_groups(i):
    return [(0, min(4, i + 1))] + ([(4, i - 3)] if i >= 4 else [])


def key_spans(i):
    w = P * (i + 1)
    return [(0, min(w, W))] + ([(W, w)] if w > W else [])


def groups_before_b(u):
    return sum(len(key_groups(v % NT)) for v in range(u))


def unit_a(u):
    return u // 16, u // 4 % 4, 4 * (u // 16) + u % 4


def groups_before_a(u):
    return sum(len(key_groups(unit_a(v)[2])) for v in range(u))


def three_pass(pe, out, lhs, rhs, start, stop):
    (lh, ll), (rh, rl) = lhs, rhs
    pe.matmul(out, lh, rh, start=start, stop=False)
    pe.matmul(out, lh, rl, start=False, stop=False)
    return pe.matmul(out, ll, rh, start=False, stop=stop)


def start_at_one(nc, semaphores):
    with nc.Block() as block:
        @block.sync
        def _(sp):
            for s in semaphores:
                sp.sem_inc(s, 1)


def layer_norm_block(nc, ctx, tag, x, xt_h, xt_l, const, ps):
    def sem(name):
        return ctx.enter_context(nc.semaphore(f"{tag}_{name}"))

    with ExitStack() as own:
        def sb(name, shape, dt=F32):
            return own.enter_context(nc.sbuf_tensor(f"{tag}_{name}", shape, dt))

        stats = sb("stats", [P, NT, 6])
        mean_var = sb("mean_var", [P, NT, 2])
        var_eps = sb("var_eps", [P, NT])
        rstd = sb("rstd", [P, NT])
        xn = sb("xn", [P, 2, C])
        stats_done = sem("stats_done")
        var_ready = sem("var_ready")
        rstd_ready = sem("rstd_ready")
        xn_ready = sem("xn_ready")
        transposed = sem("transposed")
        high_done = sem("high_done")
        low_done = sem("low_done")
        block = own.enter_context(nc.Block())

        @block.vector
        def _(dve):
            for i in range(NT):
                dve.bn_stats(stats[:, i, :], x[:, i, :]).then_inc(stats_done, 1)
            for i in range(NT):
                dve.wait_ge(stats_done, i + 1)
                dve.bn_aggr(mean_var[:, i, :], stats[:, i, :]).then_inc(stats_done, 1)
            dve.wait_ge(stats_done, 2 * NT)
            dve.tensor_scalar(var_eps[:, :], mean_var[:, :, 1], LN_EPS, None, ALU.add).then_inc(var_ready, 1)
            dve.wait_ge(rstd_ready, 1)
            for i in range(NT + 1):
                if i < NT:
                    if i >= 2:
                        dve.wait_ge(transposed, i - 1)
                    dve.tensor_scalar(xn[:, i % 2, :], x[:, i, :], mean_var[:, i, 0:1], rstd[:, i:i + 1],
                                      ALU.subtract, ALU.mult).then_inc(xn_ready, 1)
                if i >= 1:
                    j = i - 1
                    dve.wait_ge(high_done, j + 1)
                    dve.tensor_tensor(xt_l[:, :, j * P:(j + 1) * P],
                                      ps[:, 4 + j % 2, :].rearrange("p (k t) -> p k t", k=KC),
                                      xt_h[:, :, j * P:(j + 1) * P].bitcast(F32), ALU.subtract).then_inc(low_done, 1)

        @block.gpsimd
        def _(pool):
            pool.wait_ge(var_ready, 1)
            pool.tensor_tensor(rstd[:, :], var_eps[:, :], const["neg_half"][:, 0:NT], ALU.pow).then_inc(rstd_ready, 1)

        @block.tensor
        def _(pe):
            for i in range(NT):
                pe.wait_ge(xn_ready, i + 1)
                if i >= 2:
                    pe.wait_ge(low_done, i - 1)
                for k in range(KC):
                    last = pe.transpose(ps[:, 4 + i % 2, k * P:(k + 1) * P], xn[:, i % 2, k * P:(k + 1) * P],
                                        const["ident"][:, :])
                last.then_inc(transposed, 1)

        @block.scalar
        def _(act):
            for i in range(NT):
                act.wait_ge(transposed, i + 1)
                act.copy(xt_h[:, :, i * P:(i + 1) * P],
                         ps[:, 4 + i % 2, :].rearrange("p (k t) -> p k t", k=KC)).then_inc(high_done, 1)


def rotary_projection_block(nc, ctx, xt_h, xt_l, w_h, w_l, v_all, const, ps, wa_dram, parts_dram):
    def sem(name):
        return ctx.enter_context(nc.semaphore(f"pa_{name}"))

    N3 = 3 * C
    with ExitStack() as own:
        def sb(name, shape, dt=F32):
            return own.enter_context(nc.sbuf_tensor(f"pa_{name}", shape, dt))

        raw = sb("raw", [P, 2, N3])
        prod = sb("prod", [P, 2, 4, C // 2])
        rot = sb("rot", [P, 2, 2 * C])
        part = sb("part", [P, 2, 3, 2 * C], BF16)
        stage = sb("stage", [P, 2, 3, 2 * KC, 2 * P], BF16)
        w_in = [sem(f"w_in{b}") for b in range(2)]
        wh_done = sem("wh_done")
        wl_done = sem("wl_done")
        projected = sem("projected")
        prod_done = sem("prod_done")
        v_done = sem("v_done")
        rot_done = sem("rot_done")
        high_done = sem("high_done")
        rest1_done = sem("rest1_done")
        mid_done = sem("mid_done")
        low_done = sem("low_done")
        transposed = sem("transposed")
        staged = sem("staged")
        stored = [sem(f"stored{b}") for b in range(2)]
        block = own.enter_context(nc.Block())

        @block.sync
        def _(sp):
            for k in range(KC):
                if k >= 2:
                    sp.wait_ge(wl_done, k - 1)
                sp.dma_start(raw[:, k % 2, :], wa_dram[k * P:(k + 1) * P, :]).then_inc(w_in[k % 2], 16)
            for h in range(NT // 2):
                sp.wait_ge(staged, 6 * (h + 1))
                for a in range(3):
                    sp.dma_start(parts_dram[a].rearrange("(m p) t -> p m t", p=P)[:, :, 2 * h * P:2 * (h + 1) * P],
                                 stage[:, h % 2, a, :, :]).then_inc(stored[h % 2], 16)
            for b in range(2):
                sp.wait_ge(stored[b], 16 * 3 * (NT // 4))

        @block.tensor
        def _(pe):
            def project(i):
                if i == 0:
                    pe.wait_ge(wl_done, KC)
                if i >= 2:
                    pe.wait_ge(rot_done, i - 1)
                    pe.wait_ge(v_done, i - 1)
                cols = slice(i * P, (i + 1) * P)
                for k in range(KC):
                    for n in range(3):
                        last = three_pass(pe, ps[:, 3 * (i % 2) + n, :], (xt_h[:, k, cols], xt_l[:, k, cols]),
                                          (w_h[:, k, n * C:(n + 1) * C], w_l[:, k, n * C:(n + 1) * C]),
                                          k == 0, k == KC - 1)
                last.then_inc(projected, 1)

            def turn(i):
                pe.wait_ge(low_done, i + 1)
                for a in range(3):
                    n = 3 * i + a
                    if n >= 2:
                        pe.wait_ge(staged, n - 1)
                    for m in range(2 * KC):
                        last = pe.transpose(ps[:, 6 + n % 2, m * 64:(m + 1) * 64].bitcast(BF16),
                                            part[:, i % 2, a, m * P:(m + 1) * P], const["ident_bf"][:, :])
                    last.then_inc(transposed, 1)

            for i in range(NT + 1):
                if i < NT:
                    project(i)
                if i >= 1:
                    turn(i - 1)

        @block.scalar
        def _(act):
            for k in range(KC):
                act.wait_ge(w_in[k % 2], 16 * (k // 2 + 1))
                act.copy(w_h[:, k, :], raw[:, k % 2, :]).then_inc(wh_done, 1)
            for i in range(NT):
                act.wait_ge(projected, i + 1)
                if i >= 2:
                    act.wait_ge(rot_done, i - 1)
                for n in range(2):
                    odd = ps[:, 3 * (i % 2) + n, :].rearrange("p (m two) -> p m two", two=2)[:, :, 1]
                    for f in range(2):
                        last = act.activation(prod[:, i % 2, 2 * n + f, :], odd, ACT.Copy,
                                              scale=const["trig"][:, i, 2 * (1 - n) + 1 - f:2 * (1 - n) + 2 - f])
                last.then_inc(prod_done, 1)
                act.copy(v_all[:, i, :], ps[:, 3 * (i % 2) + 2, :]).then_inc(v_done, 1)
                act.wait_ge(rot_done, i + 1)
                if i >= 2:
                    act.wait_ge(transposed, 3 * (i - 1))
                act.copy(part[:, i % 2, 0, :], rot[:, i % 2, :]).then_inc(high_done, 1)
                act.wait_ge(rest1_done, i + 1)
                act.copy(part[:, i % 2, 1, :], rot[:, i % 2, :]).then_inc(mid_done, 1)

        @block.vector
        def _(dve):
            for k in range(KC):
                dve.wait_ge(wh_done, k + 1)
                dve.tensor_tensor(w_l[:, k, :], raw[:, k % 2, :], w_h[:, k, :].bitcast(F32),
                                  ALU.subtract).then_inc(wl_done, 1)

            def take(i):
                for a in range(3):
                    n = 3 * i + a
                    dve.wait_ge(transposed, n + 1)
                    if i % 2 == 0 and i >= 4:
                        dve.wait_ge(stored[i // 2 % 2], 16 * 3 * (i // 4))
                    dve.tensor_copy(stage[:, i // 2 % 2, a, :, (i % 2) * P:(i % 2 + 1) * P],
                                    ps[:, 6 + n % 2, :].bitcast(BF16).rearrange("p (m t) -> p m t", t=P)
                                    ).then_inc(staged, 1)

            for i in range(NT):
                dve.wait_ge(prod_done, i + 1)
                if i >= 2:
                    dve.wait_ge(low_done, i - 1)
                for n in range(2):
                    even = ps[:, 3 * (i % 2) + n, :].rearrange("p (m two) -> p m two", two=2)[:, :, 0]
                    out = rot[:, i % 2, n * C:(n + 1) * C].rearrange("p (m two) -> p m two", two=2)
                    cos = const["trig"][:, i, 2 * (1 - n):2 * (1 - n) + 1]
                    sin = const["trig"][:, i, 2 * (1 - n) + 1:2 * (1 - n) + 2]
                    dve.scalar_tensor_tensor(out[:, :, 0], even, cos, prod[:, i % 2, 2 * n, :], ALU.mult, ALU.subtract)
                    last = dve.scalar_tensor_tensor(out[:, :, 1], even, sin, prod[:, i % 2, 2 * n + 1, :],
                                                    ALU.mult, ALU.add)
                last.then_inc(rot_done, 1)
                if i >= 1:
                    take(i - 1)
                dve.wait_ge(high_done, i + 1)
                dve.tensor_tensor(rot[:, i % 2, :], rot[:, i % 2, :], part[:, i % 2, 0, :],
                                  ALU.subtract).then_inc(rest1_done, 1)
                dve.wait_ge(mid_done, i + 1)
                dve.tensor_tensor(part[:, i % 2, 2, :], rot[:, i % 2, :], part[:, i % 2, 1, :],
                                  ALU.subtract).then_inc(low_done, 1)
            take(NT - 1)


def rotary_attention_block(nc, ctx, v_all, o_all, const, ps, parts_dram):
    def sem(name):
        return ctx.enter_context(nc.semaphore(f"ra_{name}"))

    U = GA * NT
    NU = 2 * U
    NG = groups_before_a(U)
    HALF = U // 2
    with ExitStack() as own:
        def sb(name, shape, dt=F32):
            return own.enter_context(nc.sbuf_tensor(f"ra_{name}", shape, dt))

        q_st = [sb(f"q_st{b}", [P, GA, T], BF16) for b in range(2)]
        k_st = [sb(f"k_st{b}", [P, GA, T], BF16) for b in range(2)]
        v4 = [sb(f"v4{b}", [P, NT, GA, 32]) for b in range(2)]
        prob = sb("prob", [P, 4, T])
        pt = sb("pt", [P, GA, 8, W])
        neg_max = sb("neg_max", [P, NU])
        mask = sb("mask", [P, T])
        o_rows = sb("o_rows", [P, 2, W])
        recip = sb("recip", [P, 4, GA])
        gate = sb("gate", [P, NU])
        gate_pool = sb("gate_pool", [P, 2])
        loaded = [sem(f"loaded{b}") for b in range(2)]
        scored = sem("scored")
        shifted = sem("shifted")
        exped = sem("exped")
        turned = sem("turned")
        taken_act = sem("taken_act")
        taken_dve = sem("taken_dve")
        mixed = sem("mixed")
        rows_out = sem("rows_out")
        rows_turned = sem("rows_turned")
        recip_done = sem("recip_done")
        heads_out = sem("heads_out")
        v4_zeroed = sem("v4_zeroed")
        v4_ready = sem("v4_ready")
        mask_ready = sem("mask_ready")
        credited = [scored, shifted, exped, turned, taken_act, taken_dve, mixed, rows_out, rows_turned,
                    recip_done, heads_out, v4_ready]
        start_at_one(nc, credited)
        block = own.enter_context(nc.Block())

        def unit(v):
            return (v // U, *unit_a(v % U))

        def before(v):
            return NG * (v // U) + groups_before_a(v % U)

        def of_act(n):
            return (n + 1) // 2

        def of_dve(n):
            return n // 2

        def slot(half, j):
            return (j + 4 * half) % 8

        def take_groups(eng, copy, done, it, v, parity):
            b, half, hh, i = unit(v)
            for k, (j0, nb) in enumerate(key_groups(i)):
                n = before(v) + k
                if n % 2 != parity:
                    continue
                eng.wait_ge(turned, 1 + 2 * NG * it + n + 1)
                eng.wait_ge(mixed, 1 + 4 * it + 2 * b + (1 if half and j0 else 0))
                s0 = slot(half, j0)
                col = (i % 4) * P
                copy(pt[:, hh, s0:s0 + nb, col:col + P],
                     ps[:, 4 + n % 2, 0:nb * P].rearrange("p (j q) -> p j q", q=P)).then_inc(done, 1)

        @block.sync
        def _(sp):
            with sp.Fori(0, NGA // 2) as it:
                for b in range(2):
                    sp.wait_ge(scored, 1 + NU * it)
                    rows = [parts_dram[a].rearrange("(n g h d) t -> n g d h t", n=2, g=NGA, h=GA) for a in range(3)]
                    for s in range(SLOTS):
                        at = slice(s * DA, (s + 1) * DA)
                        for dst, n, a in ((q_st[b], 0, s // 3), (k_st[b], 1, s % 3)):
                            sp.dma_start(dst[at, :, :], rows[a][n, bass.ds(2 * it + b, 1), :, :, :].squeeze(0)
                                         ).then_inc(loaded[b], 16)

        @block.gpsimd
        def _(pool):
            for b in range(2):
                pool.memset(v4[b][:, :, :, DA + 1:32], 0.0).then_inc(v4_zeroed, 1)
                pool.memset(v4[b][:, :, :, DA:DA + 1], 1.0).then_inc(v4_zeroed, 1)
            with pool.Fori(0, NGA // 2) as it:
                for b in range(2):
                    pool.wait_ge(mixed, 1 + 4 * it)
                    pool.tensor_tensor(gate_pool[:, b:b + 1], const["neg_half"][:, 0:1], const["neg_half"][:, 0:1],
                                       ALU.add)
                    pool.tensor_copy(v4[b][:, :, :, 0:DA],
                                     v_all[:, :, bass.ds((2 * it + b) * (GA * DA), GA * DA)]
                                     .rearrange("p t (h d) -> p t h d", h=GA)).then_inc(v4_ready, 1)

        @block.tensor
        def _(pe):
            with pe.Fori(0, NGA // 2) as it:
                def score(v):
                    b, half, hh, i = unit(v)
                    if v % U == 0:
                        pe.wait_ge(loaded[b], 16 * 2 * SLOTS * (it + 1))
                    if v == 0:
                        pe.wait_ge(shifted, 1 + NU * it)
                    elif v >= 2:
                        pe.wait_ge(shifted, 1 + NU * it + v - 1)
                    for c, (k0, k1) in enumerate(key_spans(i)):
                        last = pe.matmul(ps[:, 2 * (v % 2) + c, 0:k1 - k0], q_st[b][:, hh, i * P:(i + 1) * P],
                                         k_st[b][:, hh, k0:k1], start=True, stop=True)
                    last.then_inc(scored, 1)

                def turn(v):
                    b, half, hh, i = unit(v)
                    pe.wait_ge(exped, 1 + NU * it + v + 1)
                    for k, (j0, nb) in enumerate(key_groups(i)):
                        n = before(v) + k
                        if n < 2:
                            pe.wait_ge(taken_dve if n % 2 else taken_act, 1 + NG * it)
                        else:
                            pe.wait_ge(taken_dve if n % 2 else taken_act, 1 + NG * it + n // 2)
                        for j in range(nb):
                            last = pe.transpose(ps[:, 4 + n % 2, j * P:(j + 1) * P],
                                                prob[:, v % 4, (j0 + j) * P:(j0 + j + 1) * P], const["ident"][:, :])
                        last.then_inc(turned, 1)

                def mix(job):
                    b, half = job // 2, job % 2
                    n = before(HALF * (job + 1))
                    pe.wait_ge(taken_act, 1 + NG * it + of_act(n))
                    pe.wait_ge(taken_dve, 1 + NG * it + of_dve(n))
                    pe.wait_ge(rows_out, 1 + 4 * it + job)
                    pe.wait_ge(v4_ready, 1 + 2 * it + b + 1)
                    nj = 4 * half + 4
                    for j in range(nj):
                        off = max(0, (j - 4 * half) * P)
                        for hh in range(GA):
                            last = pe.matmul(ps[32 * hh:32 * hh + 32, 6, off:W], v4[b][:, j, hh, :],
                                             pt[:, hh, slot(half, j), off:W], start=(j == 0), stop=(j == nj - 1))
                    last.then_inc(mixed, 1)

                def turn_rows(job):
                    pe.wait_ge(rows_out, 1 + 4 * it + job + 1)
                    pe.wait_ge(heads_out, 1 + 4 * it + job)
                    for t in range(4):
                        last = pe.transpose(ps[:, 7, t * P:(t + 1) * P], o_rows[:, job % 2, t * P:(t + 1) * P],
                                            const["ident"][:, :])
                    last.then_inc(rows_turned, 1)

                for s in range(NU + 4):
                    if s < NU:
                        score(s)
                    if 0 <= s - 2 < NU:
                        turn(s - 2)
                    if s >= 18 and (s - 18) % HALF == 0:
                        mix((s - 18) // HALF)
                    if s >= 19 and (s - 19) % HALF == 0:
                        turn_rows((s - 19) // HALF)

        @block.scalar
        def _(act):
            with act.Fori(0, NGA // 2) as it:
                for s in range(NU + 4):
                    if s < NU:
                        i = unit(s)[3]
                        w = P * (i + 1)
                        act.wait_ge(shifted, 1 + NU * it + s + 1)
                        act.activation(prob[:, s % 4, 0:w], prob[:, s % 4, 0:w], ACT.Exp,
                                       bias=neg_max[:, s:s + 1], scale=-1.0).then_inc(exped, 1)
                    if 0 <= s - 2 < NU:
                        take_groups(act, act.copy, taken_act, it, s - 2, 0)
                    if s >= 18 and (s - 18) % HALF == 0:
                        job = (s - 18) // HALF
                        act.wait_ge(mixed, 1 + 4 * it + job + 1)
                        act.copy(o_rows[:, job % 2, :], ps[:, 6, :]).then_inc(rows_out, 1)

        @block.vector
        def _(dve):
            dve.tensor_scalar(mask[:, :], const["rel"][:, :], 0.5 * NEG, NEG, ALU.is_le, ALU.mult).then_inc(mask_ready, 1)
            dve.wait_ge(mask_ready, 1)
            dve.wait_ge(v4_zeroed, 4)
            with dve.Fori(0, NGA // 2) as it:
                for s in range(NU + 4):
                    if s < NU:
                        i = unit(s)[3]
                        w = P * (i + 1)
                        dve.wait_ge(scored, 1 + NU * it + s + 1)
                        dve.wait_ge(turned, 1 + 2 * NG * it + (before(s - 3) if s >= 4 else 0))
                        dve.memset(gate[:, s:s + 1], 0.0)
                        dve.tensor_tensor_reduce(out=prob[:, s % 4, 0:w],
                                                 in0=ps[:, 2 * (s % 2):2 * (s % 2) + 2, :].rearrange("p a b -> p (a b)")[:, 0:w],
                                                 in1=mask[:, SLIDE - i * P:T], scale=-1.0, scalar=3e38,
                                                 op0=ALU.add, op1=ALU.min,
                                                 accum_out=neg_max[:, s:s + 1]).then_inc(shifted, 1)
                    if 0 <= s - 2 < NU:
                        take_groups(dve, dve.tensor_copy, taken_dve, it, s - 2, 1)
                    if s >= 19 and (s - 19) % HALF == 0:
                        job = (s - 19) // HALF
                        b, half = job // 2, job % 2
                        dve.wait_ge(rows_turned, 1 + 4 * it + job + 1)
                        tok = ps[:, 7, :].rearrange("p (t h d) -> p t h d", t=4, h=GA)
                        dve.reciprocal(recip[:, :, :], tok[:, :, :, DA]).then_inc(recip_done, 1)
                        dve.wait_ge(recip_done, 1 + 4 * it + job + 1)
                        dst = o_all[:, 4 * half:4 * half + 4, bass.ds((2 * it + b) * (GA * DA), GA * DA)]
                        dve.tensor_tensor(dst.rearrange("p t (h d) -> p t h d", h=GA), tok[:, :, :, 0:DA],
                                          recip[:, :, :].unsqueeze(3).to_broadcast([P, 4, GA, DA]),
                                          ALU.mult).then_inc(heads_out, 1)


def rotary_output_block(nc, ctx, x, o_all, const, ps, wo_dram):
    def sem(name):
        return ctx.enter_context(nc.semaphore(f"ro_{name}"))

    with ExitStack() as own:
        def sb(name, shape, dt=F32):
            return own.enter_context(nc.sbuf_tensor(f"ro_{name}", shape, dt))

        raw = sb("raw", [P, KC, C])
        w_h = sb("w_h", [P, KC, C], F32R)
        w_l = sb("w_l", [P, KC, C], F32R)
        ot_h = sb("ot_h", [P, KC, T], F32R)
        ot_l = sb("ot_l", [P, KC, T], F32R)
        w_in = [sem(f"w_in{k}") for k in range(KC + 1)]
        wh_done = sem("wh_done")
        wl_done = sem("wl_done")
        turned = sem("turned")
        high_done = sem("high_done")
        low_done = sem("low_done")
        projected = sem("projected")
        added = sem("added")
        block = own.enter_context(nc.Block())

        @block.sync
        def _(sp):
            for k in range(KC):
                sp.dma_start(raw[:, k, :], wo_dram[k * P:(k + 1) * P, :]).then_inc(w_in[k], 16)

        @block.tensor
        def _(pe):
            for i in range(NT + 1):
                if i < NT:
                    if i >= 2:
                        pe.wait_ge(low_done, i - 1)
                    for k in range(KC):
                        last = pe.transpose(ps[:, 4 + i % 2, k * P:(k + 1) * P], o_all[:, i, k * P:(k + 1) * P],
                                            const["ident"][:, :])
                    last.then_inc(turned, 1)
                if i >= 1:
                    j = i - 1
                    if j == 0:
                        pe.wait_ge(wl_done, KC)
                    pe.wait_ge(low_done, j + 1)
                    if j >= 2:
                        pe.wait_ge(added, j - 1)
                    for k in range(KC):
                        last = three_pass(pe, ps[:, j % 2, :], (ot_h[:, k, j * P:(j + 1) * P], ot_l[:, k, j * P:(j + 1) * P]),
                                          (w_h[:, k, :], w_l[:, k, :]), k == 0, k == KC - 1)
                    last.then_inc(projected, 1)

        @block.scalar
        def _(act):
            for k in range(KC):
                act.wait_ge(w_in[k], 16)
                act.copy(w_h[:, k, :], raw[:, k, :]).then_inc(wh_done, 1)
            for i in range(NT):
                act.wait_ge(turned, i + 1)
                act.copy(ot_h[:, :, i * P:(i + 1) * P],
                         ps[:, 4 + i % 2, :].rearrange("p (k t) -> p k t", k=KC)).then_inc(high_done, 1)

        @block.vector
        def _(dve):
            for k in range(KC):
                dve.wait_ge(wh_done, k + 1)
                dve.tensor_tensor(w_l[:, k, :], raw[:, k, :], w_h[:, k, :].bitcast(F32), ALU.subtract).then_inc(wl_done, 1)
            for i in range(NT + 1):
                if i < NT:
                    dve.wait_ge(high_done, i + 1)
                    dve.tensor_tensor(ot_l[:, :, i * P:(i + 1) * P],
                                      ps[:, 4 + i % 2, :].rearrange("p (k t) -> p k t", k=KC),
                                      ot_h[:, :, i * P:(i + 1) * P].bitcast(F32), ALU.subtract).then_inc(low_done, 1)
                if i >= 1:
                    j = i - 1
                    dve.wait_ge(projected, j + 1)
                    dve.tensor_tensor(x[:, j, :], ps[:, j % 2, :], x[:, j, :], ALU.add).then_inc(added, 1)


def ffn_block(nc, ctx, tag, x, xt_h, xt_l, const, ps, wf_dram, wb_dram, bias_dram, out_dram=None):
    def sem(name):
        return ctx.enter_context(nc.semaphore(f"{tag}_{name}"))

    N = C + ER + NE
    NA = ER + NE
    with ExitStack() as own:
        def sb(name, shape, dt=F32):
            return own.enter_context(nc.sbuf_tensor(f"{tag}_{name}", shape, dt))

        raw = sb("raw", [P, KC, N])
        raw_b = sb("raw_b", [P, C])
        bias = sb("bias", [P, C])
        w_h = sb("w_h", [P, KC, N], F32R)
        w_l = sb("w_l", [P, KC, N], F32R)
        wb_h = sb("wb_h", [P, C], F32R)
        wb_l = sb("wb_l", [P, C], F32R)
        hid = sb("hid", [P, NT, NA])
        top = sb("top", [P, NT, 8])
        top_i = sb("top_i", [P, NT, 8], U32)
        top_f = sb("top_f", [P, NT, 2])
        gap = sb("gap", [P, NT])
        gap_e = sb("gap_e", [P, NT])
        gap_s = sb("gap_s", [P, NT])
        w_top = sb("w_top", [P, NT, 2])
        sel = sb("sel", [P, 2, NT, NE])
        w_e = sb("w_e", [P, NT, NE])
        hw = sb("hw", [P, NT, ER])
        ht_h = sb("ht_h", [P, 2, P], F32R)
        ht_l = sb("ht_l", [P, 2, P], F32R)
        w_in = [sem(f"w_in{k}") for k in range(KC + 1)]
        b_in = sem("b_in")
        wh_done = sem("wh_done")
        wl_done = sem("wl_done")
        hidden = sem("hidden")
        hid_out = sem("hid_out")
        step = sem("step")
        exp_done = sem("exp_done")
        gated = sem("gated")
        turned = sem("turned")
        ht_high = sem("ht_high")
        ht_low = sem("ht_low")
        summed = sem("summed")
        biased = sem("biased")
        added = sem("added")
        stored = sem("stored")
        block = own.enter_context(nc.Block())

        @block.sync
        def _(sp):
            for k in range(KC):
                sp.dma_start(raw[:, k, :], wf_dram[k * P:(k + 1) * P, :]).then_inc(w_in[k], 16)
            sp.dma_start(raw_b[:, :], wb_dram).then_inc(w_in[KC], 16)
            sp.dma_start(bias[:, :], bias_dram.partition_broadcast(P)).then_inc(b_in, 16)
            if out_dram is not None:
                for i in range(NT):
                    sp.wait_ge(added, i + 1)
                    sp.dma_start(out_dram[i * P:(i + 1) * P, :], x[:, i, :]).then_inc(stored, 16)
                sp.wait_ge(stored, 16 * NT)

        @block.tensor
        def _(pe):
            def cols(i):
                return slice(i * P, (i + 1) * P)

            pe.wait_ge(wl_done, KC)
            for i in range(NT):
                if i >= 2:
                    pe.wait_ge(hid_out, i - 1)
                for k in range(KC):
                    last = three_pass(pe, ps[:, 4 + i % 2, 0:NA], (xt_h[:, k, cols(i)], xt_l[:, k, cols(i)]),
                                      (w_h[:, k, C:N], w_l[:, k, C:N]), k == 0, k == KC - 1)
                last.then_inc(hidden, 1)
            for i in range(NT + 1):
                if i < NT:
                    if i >= 4:
                        pe.wait_ge(added, i - 3)
                    for k in range(KC):
                        three_pass(pe, ps[:, i % 4, :], (xt_h[:, k, cols(i)], xt_l[:, k, cols(i)]),
                                   (w_h[:, k, 0:C], w_l[:, k, 0:C]), k == 0, False)
                    pe.wait_ge(gated, i + 1)
                    if i >= 2:
                        pe.wait_ge(ht_low, i - 1)
                    pe.transpose(ps[:, 6 + i % 2, 0:P], hw[:, i, :], const["ident"][:, :]).then_inc(turned, 1)
                if i >= 1:
                    j = i - 1
                    if j == 0:
                        pe.wait_ge(wl_done, KC + 1)
                    pe.wait_ge(ht_low, j + 1)
                    three_pass(pe, ps[:, j % 4, :], (ht_h[:, j % 2, :], ht_l[:, j % 2, :]),
                               (wb_h[:, :], wb_l[:, :]), False, True).then_inc(summed, 1)

        @block.scalar
        def _(act):
            for k in range(KC):
                act.wait_ge(w_in[k], 16)
                act.copy(w_h[:, k, :], raw[:, k, :]).then_inc(wh_done, 1)
            act.wait_ge(w_in[KC], 16)
            act.copy(wb_h[:, :], raw_b[:, :]).then_inc(wh_done, 1)
            for i in range(NT):
                act.wait_ge(hidden, i + 1)
                act.copy(hid[:, i, :], ps[:, 4 + i % 2, 0:NA]).then_inc(hid_out, 1)
            act.wait_ge(step, 1 + 2 * NT)
            act.activation(gap_e[:, :], gap[:, :], ACT.Exp).then_inc(exp_done, 1)
            for i in range(NT):
                act.wait_ge(turned, i + 1)
                if i >= 2:
                    act.wait_ge(summed, i - 1)
                act.copy(ht_h[:, i % 2, :], ps[:, 6 + i % 2, 0:P]).then_inc(ht_high, 1)

        @block.vector
        def _(dve):
            done = [0]

            def link(ins):
                done[0] += 1
                ins.then_inc(step, 1)
                dve.wait_ge(step, done[0])

            for k in range(KC):
                dve.wait_ge(wh_done, k + 1)
                dve.tensor_tensor(w_l[:, k, :], raw[:, k, :], w_h[:, k, :].bitcast(F32), ALU.subtract).then_inc(wl_done, 1)
            dve.wait_ge(wh_done, KC + 1)
            dve.tensor_tensor(wb_l[:, :], raw_b[:, :], wb_h[:, :].bitcast(F32), ALU.subtract).then_inc(wl_done, 1)
            dve.wait_ge(b_in, 16)
            for i in range(NT):
                dve.tensor_tensor(x[:, i, :], x[:, i, :], bias[:, :], ALU.add).then_inc(biased, 1)
            for i in range(NT):
                dve.wait_ge(hid_out, i + 1)
                link(dve.max(top[:, i, :], hid[:, i, ER:NA]))
                link(dve.max_index(top_i[:, i, :], top[:, i, :], hid[:, i, ER:NA]))
            link(dve.tensor_tensor(gap[:, :], top[:, :, 1], top[:, :, 0], ALU.subtract))
            link(dve.tensor_copy(top_f[:, :, :], top_i[:, :, 0:2]))
            dve.wait_ge(exp_done, 1)
            link(dve.tensor_scalar(gap_s[:, :], gap_e[:, :], 1.0 / SCALING, 1.0 / SCALING, ALU.mult, ALU.add))
            link(dve.reciprocal(w_top[:, :, 0], gap_s[:, :]))
            link(dve.tensor_tensor(w_top[:, :, 1], gap_e[:, :], w_top[:, :, 0], ALU.mult))
            for r in range(2):
                link(dve.tensor_tensor(sel[:, r, :, :], const["iota"][:, :].unsqueeze(1).to_broadcast([P, NT, NE]),
                                       top_f[:, :, r].unsqueeze(2).to_broadcast([P, NT, NE]), ALU.is_equal))
                link(dve.tensor_tensor(sel[:, r, :, :], sel[:, r, :, :],
                                       w_top[:, :, r].unsqueeze(2).to_broadcast([P, NT, NE]), ALU.mult))
            link(dve.tensor_tensor(w_e[:, :, :], sel[:, 0, :, :], sel[:, 1, :, :], ALU.add))
            for i in range(NT):
                dve.tensor_tensor(hw[:, i, :].rearrange("p (e r) -> p e r", e=NE),
                                  hid[:, i, 0:ER].rearrange("p (e r) -> p e r", e=NE),
                                  w_e[:, i, :].unsqueeze(2).to_broadcast([P, NE, NR]), ALU.mult).then_inc(gated, 1)
            dve.wait_ge(biased, NT)
            for i in range(NT + 1):
                if i < NT:
                    dve.wait_ge(ht_high, i + 1)
                    dve.tensor_tensor(ht_l[:, i % 2, :], ps[:, 6 + i % 2, 0:P], ht_h[:, i % 2, :].bitcast(F32),
                                      ALU.subtract).then_inc(ht_low, 1)
                if i >= 1:
                    j = i - 1
                    dve.wait_ge(summed, j + 1)
                    dve.tensor_tensor(x[:, j, :], ps[:, j % 4, :], x[:, j, :], ALU.add).then_inc(added, 1)


def alibi_attention_block(nc, ctx, x, xt_h, xt_l, const, ps, wqkv_dram, wo_dram):
    def sem(name):
        return ctx.enter_context(nc.semaphore(f"ab_{name}"))

    U = GB * NT
    NG = groups_before_b(U)
    JOBS = U // 4
    NQ = GB * DB
    NW = NQ + 2 * DB
    with ExitStack() as own:
        def sb(name, shape, dt=F32):
            return own.enter_context(nc.sbuf_tensor(f"ab_{name}", shape, dt))

        raw = sb("raw", [P, 2, NW])
        w_h = sb("w_h", [P, KC, NW], F32R)
        w_l = sb("w_l", [P, KC, NW], F32R)
        wo_h = sb("wo_h", [P, GB, C], F32R)
        wo_l = sb("wo_l", [P, GB, C], F32R)
        qt_h = sb("qt_h", [P, GB, T], F32R)
        qt_l = sb("qt_l", [P, GB, T], F32R)
        kt_h = sb("kt_h", [P, T], F32R)
        kt_l = sb("kt_l", [P, T], F32R)
        v_h = sb("v_h", [P, NT, DB], F32R)
        v_l = sb("v_l", [P, NT, DB], F32R)
        nat = sb("nat", [P, 2, GB + 1, DB])
        squares = sb("squares", [P, GB + 1, DB], BF16)
        sq_sum = sb("sq_sum", [P, NT, GB + 1])
        ms_eps = sb("ms_eps", [P, NT, GB + 1])
        rms = sb("rms", [P, NT, GB + 1])
        prob = sb("prob", [P, 3, T])
        pt_h = sb("pt_h", [P, 8, W], F32R)
        pt_l = sb("pt_l", [P, 8, W], F32R)
        bias = sb("bias", [P, T])
        neg_max = sb("neg_max", [P, U])
        sums = sb("sums", [P, U])
        recip = sb("recip", [P, U])
        gate = sb("gate", [P, U])
        gate_pool = sb("gate_pool", [P, GB + KC])
        raw_in = [sem(f"raw_in{b}") for b in range(2)]
        split = sem("split")
        split_high = sem("split_high")
        split_o = sem("split_o")
        projected = sem("projected")
        squared = sem("squared")
        ms_ready = sem("ms_ready")
        rms_ready = sem("rms_ready")
        v_high = sem("v_high")
        scaled = sem("scaled")
        qk_turned = sem("qk_turned")
        qk_high = sem("qk_high")
        qk_low = sem("qk_low")
        bias_ready = sem("bias_ready")
        scored = sem("scored")
        shifted = sem("shifted")
        exped = sem("exped")
        recip_done = sem("recip_done")
        normed = sem("normed")
        turned = sem("turned")
        pt_high = sem("pt_high")
        pt_low = sem("pt_low")
        mixed = sem("mixed")
        o_high = sem("o_high")
        o_low = sem("o_low")
        out_done = sem("out_done")
        added = sem("added")
        credited = [split, split_high, split_o, projected, squared, ms_ready, rms_ready, v_high, scaled,
                    qk_turned, qk_high, qk_low, bias_ready, scored, shifted, exped, recip_done, normed,
                    turned, pt_high, pt_low, mixed, o_high, o_low, out_done, added]
        start_at_one(nc, credited)
        block = own.enter_context(nc.Block())

        def slot(job, j):
            return (4 * (job // 2 % 2) + 4 * (job % 2) + j) % 8

        def parts_before(job):
            return 3 * (job // 2) + job % 2

        PARTS = parts_before(JOBS)

        def last_reader(job, j0):
            if job % 2 == 0:
                return max(0, parts_before(job) - 1)
            if j0 == 0:
                return parts_before(job - 1)
            return parts_before(job)

        def finished(s):
            if s >= 6 and (s - 6) % 8 == 0:
                return 2 * ((s - 6) // 8)
            if s >= 11 and (s - 11) % 8 == 0:
                return 2 * ((s - 11) // 8) + 1
            return None

        @block.sync
        def _(sp):
            def load_qkv(g, k):
                sp.dma_start(raw[:, k % 2, :], wqkv_dram[bass.ds(g, 1), k * P:(k + 1) * P, :].squeeze(0)
                             ).then_inc(raw_in[k % 2], 16)

            for k in range(KC):
                if k >= 2:
                    sp.wait_ge(split, 1 + k - 1)
                load_qkv(0, k)
            with sp.Fori(0, KVB) as g:
                for k in range(GB):
                    if k < 2:
                        sp.wait_ge(split, 1 + KC * g + KC - 1 + k)
                    else:
                        sp.wait_ge(split_o, 1 + GB * g + k - 1)
                    sp.dma_start(raw[:, k % 2, 0:C], wo_dram[bass.ds(g, 1), k * P:(k + 1) * P, :].squeeze(0)
                                 ).then_inc(raw_in[k % 2], 16)
                for k in range(KC):
                    if k < 2:
                        sp.wait_ge(split_o, 1 + GB * g + GB - 1 + k)
                    else:
                        sp.wait_ge(split, 1 + KC * g + KC + k - 1)
                    load_qkv(g + 1, k)

        @block.gpsimd
        def _(pool):
            def carry_wait(n):
                pool.tensor_tensor(gate_pool[:, n:n + 1], const["neg_half"][:, 0:1], const["neg_half"][:, 0:1], ALU.add)

            for k in range(KC):
                pool.wait_ge(raw_in[k % 2], 16 * (k // 2 + 1))
                pool.tensor_copy(w_h[:, k, :], raw[:, k % 2, :]).then_inc(split_high, 1)
                pool.wait_ge(split_high, 1 + k + 1)
                pool.tensor_tensor(w_l[:, k, :], raw[:, k % 2, :], w_h[:, k, :].bitcast(F32), ALU.subtract).then_inc(split, 1)
            with pool.Fori(0, KVB) as g:
                for i in range(NT):
                    pool.wait_ge(ms_ready, 1 + NT * g + i + 1)
                    pool.tensor_tensor(rms[:, i, :], ms_eps[:, i, :], const["neg_half"][:, 0:GB + 1], ALU.pow).then_inc(rms_ready, 1)
                pool.wait_ge(out_done, 1 + NT * g)
                for k in range(GB):
                    pool.wait_ge(raw_in[k % 2], 64 * g + 32 + 16 * (k // 2 + 1))
                    carry_wait(k)
                    pool.tensor_copy(wo_h[:, k, :], raw[:, k % 2, 0:C]).then_inc(split_high, 1)
                    pool.wait_ge(split_high, 1 + 8 * g + KC + k + 1)
                    pool.tensor_tensor(wo_l[:, k, :], raw[:, k % 2, 0:C], wo_h[:, k, :].bitcast(F32),
                                       ALU.subtract).then_inc(split_o, 1)
                pool.wait_ge(projected, 1 + NT * g + NT)
                for k in range(KC):
                    pool.wait_ge(raw_in[k % 2], 64 * g + 64 + 16 * (k // 2 + 1))
                    carry_wait(GB + k)
                    pool.tensor_copy(w_h[:, k, :], raw[:, k % 2, :]).then_inc(split_high, 1)
                    pool.wait_ge(split_high, 1 + 8 * g + KC + GB + k + 1)
                    pool.tensor_tensor(w_l[:, k, :], raw[:, k % 2, :], w_h[:, k, :].bitcast(F32),
                                       ALU.subtract).then_inc(split, 1)

        @block.tensor
        def _(pe):
            with pe.Fori(0, KVB) as g:
                def project(i):
                    if i == 0:
                        pe.wait_ge(split, 1 + KC * g + KC)
                        pe.wait_ge(shifted, 1 + U * g)
                    if i >= 2:
                        pe.wait_ge(scaled, 1 + NT * g + i - 1)
                    cols = slice(i * P, (i + 1) * P)
                    b0 = 2 * (i % 2)
                    for k in range(KC):
                        three_pass(pe, ps[:, b0, :], (xt_h[:, k, cols], xt_l[:, k, cols]),
                                   (w_h[:, k, 0:NQ], w_l[:, k, 0:NQ]), k == 0, k == KC - 1)
                        last = three_pass(pe, ps[:, b0 + 1, 0:2 * DB], (xt_h[:, k, cols], xt_l[:, k, cols]),
                                          (w_h[:, k, NQ:NW], w_l[:, k, NQ:NW]), k == 0, k == KC - 1)
                    last.then_inc(projected, 1)

                def turn_qk(i):
                    pe.wait_ge(scaled, 1 + NT * g + i + 1)
                    if i == 0:
                        pe.wait_ge(pt_low, 1 + NG * g)
                    else:
                        pe.wait_ge(qk_low, 1 + NT * g + i)
                    for h in range(GB + 1):
                        at = h * P if h < GB else 0
                        last = pe.transpose(ps[:, 4 + h // GB, at:at + P], nat[:, i % 2, h, :], const["ident"][:, :])
                    last.then_inc(qk_turned, 1)

                def score(v):
                    hh, i = v // NT, v % NT
                    if v == 0:
                        pe.wait_ge(qk_low, 1 + NT * g + NT)
                    if v >= 2:
                        pe.wait_ge(shifted, 1 + U * g + v - 1)
                    for c, (k0, k1) in enumerate(key_spans(i)):
                        last = three_pass(pe, ps[:, 2 * (v % 2) + c, 0:k1 - k0],
                                          (qt_h[:, hh, i * P:(i + 1) * P], qt_l[:, hh, i * P:(i + 1) * P]),
                                          (kt_h[:, k0:k1], kt_l[:, k0:k1]), True, True)
                    last.then_inc(scored, 1)

                def turn(v):
                    pe.wait_ge(normed, 1 + U * g + v + 1)
                    for k, (j0, nb) in enumerate(key_groups(v % NT)):
                        n = groups_before_b(v) + k
                        if n >= 2:
                            pe.wait_ge(pt_low, 1 + NG * g + n - 1)
                        for j in range(nb):
                            last = pe.transpose(ps[:, 4 + n % 2, j * P:(j + 1) * P],
                                                prob[:, v % 3, (j0 + j) * P:(j0 + j + 1) * P], const["ident"][:, :])
                        last.then_inc(turned, 1)

                def mix(job, j0):
                    half = job % 2
                    if j0 == 0:
                        pe.wait_ge(pt_low, 1 + NG * g + groups_before_b(4 * job + 4))
                        if job == 0:
                            pe.wait_ge(added, 1 + NT * g)
                        else:
                            pe.wait_ge(o_low, 1 + JOBS * g + job)
                    nj = 4 * half + 4
                    for j in range(j0, j0 + 4):
                        off = max(0, (j - 4 * half) * P)
                        s = slot(job, j)
                        last = three_pass(pe, ps[:, 6, off:W], (v_h[:, j, :], v_l[:, j, :]),
                                          (pt_h[:, s, off:W], pt_l[:, s, off:W]), j == 0, j == nj - 1)
                    last.then_inc(mixed, 1)

                def project_out(i):
                    if i == 0:
                        pe.wait_ge(o_low, 1 + JOBS * g + JOBS)
                        pe.wait_ge(split_o, 1 + GB * g + GB)
                    if i >= 2:
                        pe.wait_ge(added, 1 + NT * g + i - 1)
                    for h in range(GB):
                        last = three_pass(pe, ps[:, 6 + i % 2, :],
                                          (qt_h[:, h, i * P:(i + 1) * P], qt_l[:, h, i * P:(i + 1) * P]),
                                          (wo_h[:, h, :], wo_l[:, h, :]), h == 0, h == GB - 1)
                    last.then_inc(out_done, 1)

                for i in range(NT + 1):
                    if i < NT:
                        project(i)
                    if i >= 1:
                        turn_qk(i - 1)
                for s in range(U + 4):
                    if s < U:
                        score(s)
                    if 0 <= s - 2 < U:
                        turn(s - 2)
                    if s >= 6 and (s - 6) % 4 == 0:
                        mix((s - 6) // 4, 0)
                    if s >= 11 and (s - 11) % 8 == 0:
                        mix(2 * ((s - 11) // 8) + 1, 4)
                for i in range(NT):
                    project_out(i)

        @block.scalar
        def _(act):
            with act.Fori(0, KVB) as g:
                def squares_of(i):
                    b0 = 2 * (i % 2)
                    act.wait_ge(projected, 1 + NT * g + i + 1)
                    act.wait_ge(squared, 1 + NT * g + i)
                    for h in range(GB + 1):
                        src = ps[:, b0, h * P:(h + 1) * P] if h < GB else ps[:, b0 + 1, 0:DB]
                        last = act.activation(squares[:, h, :], src, ACT.Square, accum_out=sq_sum[:, i, h:h + 1])
                    last.then_inc(squared, 1)
                    act.copy(v_h[:, i, :], ps[:, b0 + 1, DB:2 * DB]).then_inc(v_high, 1)

                def take_qk(i):
                    act.wait_ge(qk_turned, 1 + NT * g + i + 1)
                    act.copy(qt_h[:, :, i * P:(i + 1) * P], ps[:, 4, :].rearrange("p (h t) -> p h t", h=GB))
                    act.copy(kt_h[:, i * P:(i + 1) * P], ps[:, 5, 0:P]).then_inc(qk_high, 1)

                for i in range(NT + 1):
                    if i < NT:
                        squares_of(i)
                    if i >= 1:
                        take_qk(i - 1)
                for s in range(U + 4):
                    if 0 <= s - 2 < U:
                        v = s - 2
                        job, col = v // 4, (v % 4) * P
                        for k, (j0, nb) in enumerate(key_groups(v % NT)):
                            n = groups_before_b(v) + k
                            act.wait_ge(turned, 1 + NG * g + n + 1)
                            act.wait_ge(mixed, 1 + PARTS * g + last_reader(job, j0))
                            s0 = slot(job, j0)
                            act.copy(pt_h[:, s0:s0 + nb, col:col + P],
                                     ps[:, 4 + n % 2, 0:nb * P].rearrange("p (j q) -> p j q", q=P)).then_inc(pt_high, 1)
                    if s < U:
                        w = P * (s % NT + 1)
                        act.wait_ge(shifted, 1 + U * g + s + 1)
                        act.activation(prob[:, s % 3, 0:w], prob[:, s % 3, 0:w], ACT.Exp, bias=neg_max[:, s:s + 1],
                                       scale=-1.0, accum_out=sums[:, s:s + 1]).then_inc(exped, 1)
                    job = finished(s)
                    if job is not None:
                        act.wait_ge(mixed, 1 + PARTS * g + parts_before(job + 1))
                        act.copy(qt_h[:, job // 2, job % 2 * W:(job % 2 + 1) * W], ps[:, 6, :]).then_inc(o_high, 1)

        @block.vector
        def _(dve):
            with dve.Fori(0, KVB) as g:
                def take_qk_low(i):
                    dve.wait_ge(qk_high, 1 + NT * g + i + 1)
                    cols = slice(i * P, (i + 1) * P)
                    dve.tensor_tensor(qt_l[:, :, cols], ps[:, 4, :].rearrange("p (h t) -> p h t", h=GB),
                                      qt_h[:, :, cols].bitcast(F32), ALU.subtract)
                    dve.tensor_tensor(kt_l[:, cols], ps[:, 5, 0:P], kt_h[:, cols].bitcast(F32), ALU.subtract).then_inc(qk_low, 1)

                for i in range(NT + 1):
                    if i < NT:
                        dve.wait_ge(squared, 1 + NT * g + i + 1)
                        dve.tensor_scalar(ms_eps[:, i, :], sq_sum[:, i, :], 1.0 / DB, RMS_EPS, ALU.mult, ALU.add).then_inc(ms_ready, 1)
                    if i >= 1:
                        take_qk_low(i - 1)
                    if i < NT:
                        b0 = 2 * (i % 2)
                        dve.wait_ge(rms_ready, 1 + NT * g + i + 1)
                        dve.wait_ge(v_high, 1 + NT * g + i + 1)
                        dve.tensor_tensor(nat[:, i % 2, 0:GB, :], ps[:, b0, :].rearrange("p (h d) -> p h d", h=GB),
                                          rms[:, i, 0:GB].unsqueeze(2).to_broadcast([P, GB, DB]), ALU.mult)
                        dve.scalar_tensor_tensor(nat[:, i % 2, GB, :], ps[:, b0 + 1, 0:DB], rms[:, i, GB:GB + 1],
                                                 const["w_norm"][:, :], ALU.mult, ALU.mult)
                        dve.tensor_tensor(v_l[:, i, :], ps[:, b0 + 1, DB:2 * DB], v_h[:, i, :].bitcast(F32),
                                          ALU.subtract).then_inc(scaled, 1)
                for s in range(U + 4):
                    if s < U:
                        i = s % NT
                        w = P * (i + 1)
                        if i == 0:
                            dve.wait_ge(shifted, 1 + U * g + s)
                            dve.tensor_scalar(bias[:, :], const["rel"][:, :], const["slopes"][:, bass.ds(g * GB + s // NT, 1)],
                                              None, ALU.mult).then_inc(bias_ready, 1)
                            dve.wait_ge(bias_ready, 1 + GB * g + s // NT + 1)
                        dve.wait_ge(scored, 1 + U * g + s + 1)
                        dve.wait_ge(turned, 1 + NG * g + (groups_before_b(s - 2) if s >= 3 else 0))
                        dve.memset(gate[:, s:s + 1], 0.0)
                        dve.tensor_tensor_reduce(out=prob[:, s % 3, 0:w],
                                                 in0=ps[:, 2 * (s % 2):2 * (s % 2) + 2, :].rearrange("p a b -> p (a b)")[:, 0:w],
                                                 in1=bias[:, SLIDE - i * P:T], scale=-1.0, scalar=3e38,
                                                 op0=ALU.add, op1=ALU.min,
                                                 accum_out=neg_max[:, s:s + 1]).then_inc(shifted, 1)
                    if 0 <= s - 1 < U:
                        v = s - 1
                        w = P * (v % NT + 1)
                        dve.wait_ge(exped, 1 + U * g + v + 1)
                        dve.reciprocal(recip[:, v:v + 1], sums[:, v:v + 1]).then_inc(recip_done, 1)
                        dve.wait_ge(recip_done, 1 + U * g + v + 1)
                        dve.tensor_scalar(prob[:, v % 3, 0:w], prob[:, v % 3, 0:w], recip[:, v:v + 1], None,
                                          ALU.mult).then_inc(normed, 1)
                    if 0 <= s - 2 < U:
                        v = s - 2
                        col = (v % 4) * P
                        for k, (j0, nb) in enumerate(key_groups(v % NT)):
                            n = groups_before_b(v) + k
                            s0 = slot(v // 4, j0)
                            dve.wait_ge(pt_high, 1 + NG * g + n + 1)
                            dve.tensor_tensor(pt_l[:, s0:s0 + nb, col:col + P],
                                              ps[:, 4 + n % 2, 0:nb * P].rearrange("p (j q) -> p j q", q=P),
                                              pt_h[:, s0:s0 + nb, col:col + P].bitcast(F32),
                                              ALU.subtract).then_inc(pt_low, 1)
                    job = finished(s)
                    if job is not None:
                        at = slice(job % 2 * W, (job % 2 + 1) * W)
                        dve.wait_ge(o_high, 1 + JOBS * g + job + 1)
                        dve.tensor_tensor(qt_l[:, job // 2, at], ps[:, 6, :], qt_h[:, job // 2, at].bitcast(F32),
                                          ALU.subtract).then_inc(o_low, 1)
                for i in range(NT):
                    if i == 0:
                        dve.wait_ge(added, 1 + NT * g)
                    dve.wait_ge(out_done, 1 + NT * g + i + 1)
                    dve.tensor_tensor(x[:, i, :], ps[:, 6 + i % 2, :], x[:, i, :], ALU.add).then_inc(added, 1)


def hybrid_layer_kernel(nc, ins, out_dram):
    with ExitStack() as ctx:
        def sb(name, shape, dt=F32):
            return ctx.enter_context(nc.sbuf_tensor(name, shape, dt))

        x = sb("x", [P, NT, C])
        const = {
            "ident": sb("ident", [P, P]),
            "ident_bf": sb("ident_bf", [P, P], BF16),
            "rel": sb("rel", [P, T]),
            "trig": sb("trig", [P, NT, 4]),
            "slopes": sb("slopes", [P, HB]),
            "iota": sb("iota", [P, NE]),
            "neg_half": sb("neg_half", [P, NT]),
            "w_norm": sb("w_norm", [P, DB]),
        }
        w_norm2 = sb("w_norm2", [P, 2, DB])
        ps = ctx.enter_context(nc.psum_tensor("ps", [P, 8, W], F32))
        parts_dram = [nc.dram_tensor(f"parts{a}", [2 * C, T], BF16, kind="Internal").ap() for a in range(3)]
        loaded = ctx.enter_context(nc.semaphore("const_loaded"))
        made = ctx.enter_context(nc.semaphore("const_made"))

        with nc.Block() as block:
            @block.sync
            def _(sp):
                for i in range(NT):
                    sp.dma_start(x[:, i, :], ins["x"][i * P:(i + 1) * P, :]).then_inc(loaded, 16)
                for name in ("ident", "rel", "trig", "slopes", "iota"):
                    sp.dma_start(const[name][:], ins[name]).then_inc(loaded, 16)
                sp.dma_start(w_norm2[:, :, :], ins["w_norm"].partition_broadcast(P)).then_inc(loaded, 16)
                sp.wait_ge(loaded, 16 * (NT + 6))

            @block.vector
            def _(dve):
                dve.memset(const["neg_half"][:, :], -0.5)
                dve.wait_ge(loaded, 16 * (NT + 6))
                dve.tensor_copy(const["ident_bf"][:, :], const["ident"][:, :])
                dve.scalar_tensor_tensor(const["w_norm"][:, :], w_norm2[:, 0, :], DB ** -0.5, w_norm2[:, 1, :],
                                         ALU.mult, ALU.mult).then_inc(made, 1)
                dve.wait_ge(made, 1)

        def with_xt(tag, use):
            with ExitStack() as own:
                xt_h = own.enter_context(nc.sbuf_tensor(f"{tag}_xt_h", [P, KC, T], F32R))
                xt_l = own.enter_context(nc.sbuf_tensor(f"{tag}_xt_l", [P, KC, T], F32R))
                layer_norm_block(nc, ctx, f"{tag}n", x, xt_h, xt_l, const, ps)
                use(xt_h, xt_l)

        with ExitStack() as rotary:
            v_all = rotary.enter_context(nc.sbuf_tensor("v_all", [P, NT, C], F32))

            def project(xt_h, xt_l):
                with ExitStack() as own:
                    w_h = own.enter_context(nc.sbuf_tensor("wa_h", [P, KC, 3 * C], F32R))
                    w_l = own.enter_context(nc.sbuf_tensor("wa_l", [P, KC, 3 * C], F32R))
                    rotary_projection_block(nc, ctx, xt_h, xt_l, w_h, w_l, v_all, const, ps, ins["wa"], parts_dram)

            with_xt("a", project)
            o_all = rotary.enter_context(nc.sbuf_tensor("o_all", [P, NT, C], F32))
            rotary_attention_block(nc, ctx, v_all, o_all, const, ps, parts_dram)
            rotary_output_block(nc, ctx, x, o_all, const, ps, ins["wao"])
        with_xt("f1", lambda h, l: ffn_block(nc, ctx, "f1", x, h, l, const, ps, ins["wf"], ins["wb"], ins["bf"]))
        with_xt("b", lambda h, l: alibi_attention_block(nc, ctx, x, h, l, const, ps, ins["wqkv"], ins["wbo"]))
        with_xt("f2", lambda h, l: ffn_block(nc, ctx, "f2", x, h, l, const, ps, ins["wf"], ins["wb"], ins["bf"], out_dram))



def tables():
    p = np.arange(P, dtype=np.float32)[:, None]
    rel = np.arange(T, dtype=np.float32)[None, :] - np.float32(SLIDE) - p
    rel = np.where(rel > 0, np.float32(NEG), rel).astype(np.float32)
    theta = (np.arange(NT, dtype=np.float32)[None, :] * P + p)
    cos, sin = np.cos(theta), np.sin(theta)
    scale = np.float32(DA ** -0.5)
    trig = np.stack([cos, sin, cos * scale, sin * scale], axis=-1).astype(np.float32)
    start = 2.0 ** (-2.0 ** (-(np.log2(HB) - 3)))
    slopes = np.array([start * start ** i for i in range(HB)], dtype=np.float32)
    return {
        "ident": np.eye(P, dtype=np.float32),
        "rel": rel,
        "trig": trig,
        "slopes": np.tile(slopes[None, :], (P, 1)),
        "iota": np.tile(np.arange(NE, dtype=np.float32)[None, :], (P, 1)),
    }


def layouts(i):
    wq = np.asarray(i["L0_attn_b_Wq"]).reshape(KVB, GB * DB, C)
    wk = np.asarray(i["L0_attn_b_Wk"]).reshape(KVB, DB, C)
    wv = np.asarray(i["L0_attn_b_Wv"]).reshape(KVB, DB, C)
    qkv = np.concatenate([wq, wk, wv], axis=1).transpose(0, 2, 1)
    qkv = np.concatenate([qkv, np.zeros_like(qkv[:1])], axis=0)
    a = [np.asarray(i[f"L0_attn_a_{n}"]) for n in ("wq", "wk", "wv")]
    lora_a = np.asarray(i["L0_ffn_lora_A"]).reshape(ER, C)
    return {
        "x": np.asarray(i["L0_attn_a_x"]).reshape(T, C),
        "wa": np.concatenate([w.T for w in a], axis=1),
        "wao": np.asarray(i["L0_attn_a_wo"]).T,
        "wqkv": qkv,
        "wbo": np.asarray(i["L0_attn_b_Wo"]).T.reshape(KVB, GB * DB, C),
        "w_norm": np.stack([np.asarray(i["L0_attn_b_q_norm_w"]), np.asarray(i["L0_attn_b_k_norm_w"])]),
        "wf": np.concatenate([np.asarray(i["L0_ffn_W_base"]), lora_a, np.asarray(i["L0_ffn_W_router"])], axis=0).T,
        "wb": np.asarray(i["L0_ffn_lora_B"]).transpose(0, 2, 1).reshape(ER, C),
        "bf": np.asarray(i["L0_ffn_b_base"]),
    }


def kernel(**inputs):
    import concourse.bacc as bacc
    from concourse.bass_utils import run_bass_kernel_spmd

    arrays = {n: np.ascontiguousarray(a) for n, a in {**layouts(inputs), **tables()}.items()}
    nc = bacc.Bacc("TRN2", target_bir_lowering=False, num_devices=1)
    ins = {n: nc.dram_tensor(f"in_{n}", a.shape, mybir.dt.from_np(a.dtype), kind="ExternalInput").ap()
           for n, a in arrays.items()}
    out = nc.dram_tensor("out_0_dram", (T, C), F32, kind="ExternalOutput").ap()
    hybrid_layer_kernel(nc, ins, out)
    r = run_bass_kernel_spmd(nc, [{f"in_{n}": a for n, a in arrays.items()}], core_ids=[0])
    return r.results[0]["out_0_dram"].reshape(1, T, C)
```

```python
from contextlib import ExitStack

import numpy as np

import concourse.bass as bass
from concourse import mybir

F32 = mybir.dt.float32
F32R = mybir.dt.float32r
BF16 = mybir.dt.bfloat16
U32 = mybir.dt.uint32
ALU = mybir.AluOpType
ACT = mybir.ActivationFunctionType
AX = mybir.AxisListType

P = 128
T = 1024
C = 512
NT = T // P
KC = C // P
W = 512
LN_EPS = 1e-5

HA, DA = 32, 16
GA = 4
NGA = HA // GA

HB, KVB, DB = 32, 8, 128
GB = HB // KVB
RMS_EPS = 1e-6

NE, NR = 8, 16
ER = NE * NR
SCALING = 32.0 / 16.0

NEG = -1e30
SLIDE = T - P


def key_groups(i):
    return [(0, min(4, i + 1))] + ([(4, i - 3)] if i >= 4 else [])


def key_spans(i):
    w = P * (i + 1)
    return [(0, min(w, W))] + ([(W, w)] if w > W else [])


def groups_before_b(u):
    return sum(len(key_groups(v % NT)) for v in range(u))


def three_pass(pe, out, lhs, rhs, start, stop):
    (lh, ll), (rh, rl) = lhs, rhs
    pe.matmul(out, lh, rh, start=start, stop=False)
    pe.matmul(out, lh, rl, start=False, stop=False)
    return pe.matmul(out, ll, rh, start=False, stop=stop)


def start_at_one(sp, semaphores):
    for s in semaphores.values():
        sp.sem_inc(s, 1)


ROTARY_CREDITED = ("piece_scored", "piece_max", "link", "max_turned", "max_out", "scored", "exped", "mixed",
                   "rows_out", "rows_turned", "recip_done", "heads_out", "v4_ready")
ALIBI_CREDITED = ("split", "split_high", "split_o", "projected", "squared", "ms_ready", "rms_ready", "v_high",
                  "scaled", "qk_turned", "qk_high", "qk_low", "bias_ready", "scored", "shifted", "exped",
                  "recip_done", "turned", "pt_high", "pt_low", "mixed", "o_out",
                  "o_high", "o_low", "out_done", "added")


def take_stats(dve, stats, x, i):
    tile, done = stats
    dve.bn_stats(tile[:, i, :], x[:, i, :]).then_inc(done, 1)


class LayerNorm:

    def __init__(self, nc, ctx, own, tag, x, xt_h, xt_l, weights, const, ps, banks=(4, 5, 6), apart=False,
                 stats=None):
        def sb(name, shape, dt=F32):
            return own.enter_context(nc.sbuf_tensor(f"{tag}_{name}", shape, dt))

        def sem(name):
            return ctx.enter_context(nc.semaphore(f"{tag}_{name}"))

        self.x, self.xt_h, self.xt_l, self.weights, self.const = x, xt_h, xt_l, weights, const
        self.apart = apart
        self.stats_given = stats is not None
        self.bank = [ps[:, b, :] for b in banks]
        self.stats, self.stats_done = stats or (sb("stats", [P, NT, 6]), sem("stats_done"))
        self.mean_var = sb("mean_var", [P, NT, 2])
        self.var_eps = sb("var_eps", [P, NT])
        self.rstd = sb("rstd", [P, NT])
        self.xn = sb("xn", [P, len(banks), C])
        self.raw = [sb(f"raw{k}", [P, src.shape[-1]]) for k, (src, _, _) in enumerate(weights)]
        self.raw_in = [sem(f"raw_in{k}") for k in range(len(weights) if apart else 1)]
        self.w_high = sem("w_high")
        self.w_low = sem("w_low")
        self.var_ready = sem("var_ready")
        self.rstd_ready = sem("rstd_ready")
        self.xn_ready = sem("xn_ready")
        self.transposed = sem("transposed")
        self.high_done = sem("high_done")
        self.low_done = sem("low_done")

    def load_weights(self, sp):
        for k, (src, _, _) in enumerate(self.weights):
            sp.dma_start(self.raw[k][:, :], src).then_inc(self.raw_in[k if self.apart else 0], 16)

    def on_vector(self, dve, x_in=()):
        x, xn, mean_var, rstd = self.x, self.xn, self.mean_var, self.rstd
        if not self.stats_given:
            for i in range(NT):
                if x_in and i % (NT // len(x_in)) == 0:
                    dve.wait_ge(x_in[i * len(x_in) // NT], 16 * NT // len(x_in))
                take_stats(dve, (self.stats, self.stats_done), x, i)
        for i in range(NT):
            dve.wait_ge(self.stats_done, i + 1)
            dve.bn_aggr(mean_var[:, i, :], self.stats[:, i, :]).then_inc(self.stats_done, 1)
        dve.wait_ge(self.stats_done, 2 * NT)
        dve.tensor_scalar(self.var_eps[:, :], mean_var[:, :, 1], LN_EPS, None, ALU.add).then_inc(self.var_ready, 1)
        dve.wait_ge(self.rstd_ready, 1)
        nb = len(self.bank)
        for i in range(NT + 2):
            if i < NT:
                if i >= nb:
                    dve.wait_ge(self.transposed, i - nb + 1)
                dve.tensor_scalar(xn[:, i % nb, :], x[:, i, :], mean_var[:, i, 0:1], rstd[:, i:i + 1],
                                  ALU.subtract, ALU.mult).then_inc(self.xn_ready, 1)
            if i >= 2:
                j = i - 2
                dve.wait_ge(self.high_done, j + 1)
                dve.tensor_tensor(self.xt_l[:, :, j * P:(j + 1) * P],
                                  self.bank[j % nb].rearrange("p (k t) -> p k t", k=KC),
                                  self.xt_h[:, :, j * P:(j + 1) * P].bitcast(F32), ALU.subtract).then_inc(self.low_done, 1)

    def on_pool(self, pool):
        for k, (_, high, low) in enumerate(self.weights):
            if k == 0:
                pool.wait_ge(self.var_ready, 1)
                pool.tensor_tensor(self.rstd[:, :], self.var_eps[:, :], self.const["neg_half"][:, 0:NT],
                                   ALU.pow).then_inc(self.rstd_ready, 1)
            pool.wait_ge(self.w_high, k + 1)
            pool.tensor_tensor(low, self.raw[k][:, :], high.bitcast(F32), ALU.subtract).then_inc(self.w_low, 1)

    def turn(self, pe, i):
        pe.wait_ge(self.xn_ready, i + 1)
        nb = len(self.bank)
        if i >= nb:
            pe.wait_ge(self.low_done, i - nb + 1)
        for k in range(KC):
            last = pe.transpose(self.bank[i % nb][:, k * P:(k + 1) * P], self.xn[:, i % nb, k * P:(k + 1) * P],
                                self.const["ident"][:, :])
        last.then_inc(self.transposed, 1)

    def split_weights(self, act, first=0, end=None):
        for k in list(range(len(self.weights)))[first:end]:
            high = self.weights[k][1]
            if self.apart:
                act.wait_ge(self.raw_in[k], 16)
            elif k == 0:
                act.wait_ge(self.raw_in[0], 16 * len(self.weights))
            act.copy(high, self.raw[k][:, :]).then_inc(self.w_high, 1)

    def take(self, act, i):
        act.wait_ge(self.transposed, i + 1)
        act.copy(self.xt_h[:, :, i * P:(i + 1) * P],
                 self.bank[i % len(self.bank)].rearrange("p (k t) -> p k t", k=KC)).then_inc(self.high_done, 1)


def layer_norm_block(nc, ctx, tag, x, xt_h, xt_l, weights, credited, const, ps, **options):
    with ExitStack() as own:
        norm = LayerNorm(nc, ctx, own, tag, x, xt_h, xt_l, weights, const, ps, **options)
        block = own.enter_context(nc.Block())

        @block.sync
        def _(sp):
            norm.load_weights(sp)
            start_at_one(sp, credited)

        @block.vector
        def _(dve):
            norm.on_vector(dve)

        @block.gpsimd
        def _(pool):
            norm.on_pool(pool)

        @block.tensor
        def _(pe):
            for i in range(NT):
                norm.turn(pe, i)

        @block.scalar
        def _(act):
            for i in range(NT):
                norm.take(act, i)
                norm.split_weights(act, i, i + 1)


def rotary_projection_block(nc, ctx, norm, xt_h, xt_l, w_h, w_l, v_all, credited, const, ps, parts_dram, x_in):
    def sem(name):
        return ctx.enter_context(nc.semaphore(f"pa_{name}"))

    with ExitStack() as own:
        def sb(name, shape, dt=F32):
            return own.enter_context(nc.sbuf_tensor(f"pa_{name}", shape, dt))

        prod = sb("prod", [P, 2, 4, C // 2])
        rot = sb("rot", [P, 2, 2 * C])
        part = sb("part", [P, 2, 3, 2 * C], BF16)
        stage = sb("stage", [P, 2, 3, 2 * KC, 2 * P], BF16)
        projected = sem("projected")
        prod_done = sem("prod_done")
        v_done = sem("v_done")
        rot_done = sem("rot_done")
        high_done = sem("high_done")
        rest1_done = sem("rest1_done")
        mid_done = sem("mid_done")
        low_done = sem("low_done")
        transposed = sem("transposed")
        staged_dve = sem("staged_dve")
        staged_act = sem("staged_act")
        stored = [sem(f"stored{b}") for b in range(2)]
        block = own.enter_context(nc.Block())

        def take_part(eng, copy, done, i, a):
            n = 3 * i + a
            eng.wait_ge(transposed, n + 1)
            if i % 2 == 0 and i >= 4:
                eng.wait_ge(stored[i // 2 % 2], 16 * 6 * (i // 4))
            copy(stage[:, i // 2 % 2, a, :, (i % 2) * P:(i % 2 + 1) * P],
                 ps[:, 6 + n % 2, :].bitcast(BF16).rearrange("p (m t) -> p m t", t=P)).then_inc(done, 1)

        @block.sync
        def _(sp):
            start_at_one(sp, credited)
            for h in range(NT // 2):
                sp.wait_ge(staged_dve, 2 * (h + 1))
                sp.wait_ge(staged_act, 4 * (h + 1))
                for a in range(3):
                    for n in range(2):
                        rows = parts_dram[a].rearrange("(n m p) t -> n p m t", n=2, p=P)
                        sp.dma_start(rows[n, :, 0:KC, 2 * h * P:2 * (h + 1) * P],
                                     stage[:, h % 2, a, n * KC:(n + 1) * KC, :]).then_inc(stored[h % 2], 16)
            for b in range(2):
                sp.wait_ge(stored[b], 16 * 6 * (NT // 4))

        @block.gpsimd
        def _(pool):
            norm.on_pool(pool)

        @block.tensor
        def _(pe):
            def project(i):
                if i >= 2:
                    pe.wait_ge(rot_done, i - 1)
                    pe.wait_ge(v_done, i - 1)
                cols = slice(i * P, (i + 1) * P)
                pe.wait_ge(norm.low_done, 1 if i == 0 else NT)
                for k in range(KC):
                    if i == 0:
                        pe.wait_ge(norm.w_low, k + 1)
                    for n in range(3):
                        last = three_pass(pe, ps[:, 3 * (i % 2) + n, :], (xt_h[:, k, cols], xt_l[:, k, cols]),
                                          (w_h[:, k, n * C:(n + 1) * C], w_l[:, k, n * C:(n + 1) * C]),
                                          k == 0, k == KC - 1)
                    if i == 0:
                        for j in range(1 + 2 * k, min(3 + 2 * k, NT)):
                            norm.turn(pe, j)
                last.then_inc(projected, 1)

            def turn(i):
                pe.wait_ge(low_done, i + 1)
                for a in range(3):
                    n = 3 * i + a
                    if a == 2:
                        pe.wait_ge(staged_dve, i + 1)
                    elif i >= 1:
                        pe.wait_ge(staged_act, 2 * i - 1 + a)
                    for m in range(2 * KC):
                        last = pe.transpose(ps[:, 6 + n % 2, m * 64:(m + 1) * 64].bitcast(BF16),
                                            part[:, i % 2, a, m * P:(m + 1) * P], const["ident_bf"][:, :])
                    last.then_inc(transposed, 1)

            norm.turn(pe, 0)
            for i in range(NT + 1):
                if i < NT:
                    project(i)
                if i >= 1:
                    turn(i - 1)

        @block.scalar
        def _(act):
            norm.split_weights(act, 0, 2)
            for i in range(NT):
                norm.take(act, i)
                if i < 2:
                    norm.split_weights(act, 2 + i, 3 + i)
            for i in range(NT):
                act.wait_ge(projected, i + 1)
                if i >= 2:
                    act.wait_ge(rot_done, i - 1)
                for n in range(2):
                    odd = ps[:, 3 * (i % 2) + n, :].rearrange("p (m two) -> p m two", two=2)[:, :, 1]
                    for f in range(2):
                        last = act.activation(prod[:, i % 2, 2 * n + f, :], odd, ACT.Copy,
                                              scale=const["trig"][:, i, 2 * (1 - n) + 1 - f:2 * (1 - n) + 2 - f])
                last.then_inc(prod_done, 1)
                act.copy(v_all[:, i, :], ps[:, 3 * (i % 2) + 2, :]).then_inc(v_done, 1)
                act.wait_ge(rot_done, i + 1)
                if i >= 2:
                    act.wait_ge(transposed, 3 * (i - 1))
                act.copy(part[:, i % 2, 0, :], rot[:, i % 2, :]).then_inc(high_done, 1)
                if i >= 1:
                    take_part(act, act.copy, staged_act, i - 1, 1)
                act.wait_ge(rest1_done, i + 1)
                act.copy(part[:, i % 2, 1, :], rot[:, i % 2, :]).then_inc(mid_done, 1)
                if i >= 1:
                    take_part(act, act.copy, staged_act, i - 1, 2)
            take_part(act, act.copy, staged_act, NT - 1, 1)
            take_part(act, act.copy, staged_act, NT - 1, 2)

        @block.vector
        def _(dve):
            norm.on_vector(dve, x_in)

            for i in range(NT):
                if i >= 1:
                    take_part(dve, dve.tensor_copy, staged_dve, i - 1, 0)
                dve.wait_ge(prod_done, i + 1)
                if i >= 2:
                    dve.wait_ge(low_done, i - 1)
                for n in range(2):
                    even = ps[:, 3 * (i % 2) + n, :].rearrange("p (m two) -> p m two", two=2)[:, :, 0]
                    out = rot[:, i % 2, n * C:(n + 1) * C].rearrange("p (m two) -> p m two", two=2)
                    cos = const["trig"][:, i, 2 * (1 - n):2 * (1 - n) + 1]
                    sin = const["trig"][:, i, 2 * (1 - n) + 1:2 * (1 - n) + 2]
                    dve.scalar_tensor_tensor(out[:, :, 0], even, cos, prod[:, i % 2, 2 * n, :], ALU.mult, ALU.subtract)
                    last = dve.scalar_tensor_tensor(out[:, :, 1], even, sin, prod[:, i % 2, 2 * n + 1, :],
                                                    ALU.mult, ALU.add)
                last.then_inc(rot_done, 1)
                dve.wait_ge(high_done, i + 1)
                dve.tensor_tensor(rot[:, i % 2, :], rot[:, i % 2, :], part[:, i % 2, 0, :],
                                  ALU.subtract).then_inc(rest1_done, 1)
                dve.wait_ge(mid_done, i + 1)
                dve.tensor_tensor(part[:, i % 2, 2, :], rot[:, i % 2, :], part[:, i % 2, 1, :],
                                  ALU.subtract).then_inc(low_done, 1)
            take_part(dve, dve.tensor_copy, staged_dve, NT - 1, 0)


A_SETS = [("edge", 0, 0), ("rest", 0, 2), ("full", 1, 0), ("full", 1, 2), ("edge", 1, 4), ("rest", 1, 6)]
A_STEPS = [(k, h) for k, (kind, _, _) in enumerate(A_SETS) for h in (range(0, GA, 2) if kind == "rest" else range(GA))]
A_SET_END = [max(t for t, (k, _) in enumerate(A_STEPS) if k == n) for n in range(len(A_SETS))]
A_BODY = 4
A_PARTS = 3
A_ROWS = 6 * DA


def blocks_a(k):
    kind, _, j = A_SETS[k]
    return {"edge": [(j, 0, 0), (j + 1, P, W + P), (j + 3, 3 * P, W)],
            "rest": [(j, 2 * P, 0)],
            "full": [(j, 0, 0), (j + 1, 0, W)]}[kind]


def rotary_attention_block(nc, ctx, v_all, o_all, wo_h, wo_l, credited, const, ps, parts_dram, wo_dram):
    def sem(name):
        return credited[name] if name in credited else ctx.enter_context(nc.semaphore(f"ra_{name}"))

    S = len(A_STEPS)
    SETS = len(A_SETS)
    UNITS = GA * NT
    PIECES = [(hh, i, c, span) for hh in range(GA) for i in range(NT) for c, span in enumerate(key_spans(i))]
    NP = len(PIECES)
    LAST_PIECE = 17
    SPLIT_AT, MAX_AT = 17, 18
    ROWS = A_ROWS + A_PARTS
    LINKS = 5
    FIRST_BANKS = (0, 1, 2, 3, 4, 5)
    PIECE_BANKS = (4, 5, 7)
    SHIFT = 6
    with ExitStack() as own:
        def sb(name, shape, dt=F32):
            return own.enter_context(nc.sbuf_tensor(f"ra_{name}", shape, dt))

        q_st = [sb(f"q_st{b}", [P, GA, T], BF16) for b in range(A_BODY)]
        k_st = [sb(f"k_st{b}", [P, GA, T], BF16) for b in range(A_BODY)]
        v4 = [sb(f"v4{b}", [P, NT, GA, 32]) for b in range(2)]
        pt = sb("pt", [P, 3, GA, 2 * W])
        mask = sb("mask", [P, P], BF16)
        part_max = sb("part_max", [P, 2, UNITS])
        row_max = sb("row_max", [P, UNITS])
        max_rest = sb("max_rest", [P, UNITS])
        max_part = sb("max_part", [P, A_PARTS, UNITS], BF16)
        max_rows = sb("max_rows", [P, P], BF16)
        o_rows = sb("o_rows", [P, 2, W])
        recip = sb("recip", [P, 4, GA])
        gate_pool = sb("gate_pool", [P, 2])
        wo_raw = sb("wo_raw", [P, 2, C])
        wo_in = [sem(f"wo_in{k}") for k in range(KC)]
        wo_high = sem("wo_high")
        wo_low = sem("wo_low")
        copied = sem("copied")
        half_loaded = sem("half_loaded")
        loaded = [sem(f"loaded{b}") for b in range(A_BODY)]
        max_in = [sem(f"max_in{b}") for b in range(A_BODY)]
        made = sem("made")
        piece_scored = sem("piece_scored")
        piece_max = sem("piece_max")
        link = sem("link")
        max_turned = sem("max_turned")
        max_out = sem("max_out")
        scored = sem("scored")
        exped = sem("exped")
        mixed = sem("mixed")
        rows_out = sem("rows_out")
        rows_turned = sem("rows_turned")
        recip_done = sem("recip_done")
        heads_out = sem("heads_out")
        v4_zeroed = sem("v4_zeroed")
        ones_made = sem("ones_made")
        v4_ready = sem("v4_ready")
        block = own.enter_context(nc.Block())

        def count(each, it, g, n):
            return 1 + A_BODY * each * it + each * g + n

        def pieces_before(t):
            total = sum(k1 - k0 + W // 4 for _, _, _, (k0, k1) in PIECES)
            n, width = 0, 0
            while n < NP and width * LAST_PIECE < t * total:
                width += PIECES[n][3][1] - PIECES[n][3][0] + W // 4
                n += 1
            return n

        def jobs_at(tau, lag):
            return [(g, half) for g in range(A_BODY) for half in range(2)
                    if S * g + A_SET_END[1 if half == 0 else SETS - 1] + 2 + lag == tau]

        @block.sync
        def _(sp):
            def load(b, group, heads=slice(0, GA), done=None):
                rows = [parts_dram[a].rearrange("(n g h d) t -> n g d h t", n=2, g=NGA + 2, h=GA) for a in range(A_PARTS)]
                for s, (qa, ka) in enumerate(((0, 0), (0, 1), (0, 2), (1, 0), (1, 1), (2, 0))):
                    at = slice(s * DA, (s + 1) * DA)
                    for dst, n, a in ((q_st[b], 0, qa), (k_st[b], 1, ka)):
                        src = rows[a][n, group] if isinstance(group, int) else rows[a][n, bass.ds(group, 1)].squeeze(0)
                        sp.dma_start(dst[at, heads, :], src[:, heads, :]).then_inc(done or loaded[b], 16)

            def load_wo(k):
                sp.dma_start(wo_raw[:, k % 2, :], wo_dram[k * P:(k + 1) * P, :]).then_inc(wo_in[k], 16)

            def store_max(b):
                for a in range(A_PARTS):
                    sp.dma_start(q_st[b][A_ROWS + a:A_ROWS + a + 1, :, :],
                                 max_rows[a * UNITS:(a + 1) * UNITS, :]).then_inc(max_in[b], 16)

            load(0, 0, slice(0, GA // 2), half_loaded)
            load(0, 0, slice(GA // 2, GA))
            load(1, 1)
            load_wo(0)
            load_wo(1)
            for a in range(A_PARTS):
                rows = parts_dram[a].rearrange("(n r) t -> n r t", n=2)
                sp.dma_start(rows[:, C:C + 2 * GA * DA, :], rows[:, 0:2 * GA * DA, :]).then_inc(copied, 16)
            sp.wait_ge(max_out, 1 + 1)
            store_max(0)
            sp.wait_ge(copied, 16 * A_PARTS)
            with sp.Fori(0, NGA // A_BODY) as it:
                for g in range(A_BODY):
                    sp.wait_ge(scored, count(S, it, max(0, g - 1), 0))
                    load((g + 2) % A_BODY, A_BODY * it + g + 2)
                    sp.wait_ge(max_out, count(1, it, g + 1, 1))
                    store_max((g + 1) % A_BODY)
            for b in range(A_BODY):
                sp.wait_ge(loaded[b], 16 * 12 * (3 if b < 2 else 2))
            sp.wait_ge(max_in[0], 16 * A_PARTS * 3)
            for k in range(2, KC):
                sp.wait_ge(wo_low, k - 1)
                load_wo(k)

        @block.gpsimd
        def _(pool):
            for b in range(2):
                pool.memset(v4[b][:, :, :, DA + 1:32], 0.0).then_inc(v4_zeroed, 1)
                pool.memset(v4[b][:, :, :, DA:DA + 1], 1.0).then_inc(v4_zeroed, 1)
            pool.wait_ge(v4_zeroed, 4)
            for b in range(A_BODY):
                pool.memset(k_st[b][A_ROWS:ROWS, :, :], 1.0).then_inc(ones_made, 1)
                pool.wait_ge(ones_made, b + 1)
            with pool.Fori(0, NGA // A_BODY) as it:
                for g in range(A_BODY):
                    pool.wait_ge(mixed, count(SETS, it, max(0, g - 1), 0))
                    pool.tensor_tensor(gate_pool[:, g % 2:g % 2 + 1], const["neg_half"][:, 0:1],
                                       const["neg_half"][:, 0:1], ALU.add)
                    pool.tensor_copy(v4[g % 2][:, :, :, 0:DA],
                                     v_all[:, :, bass.ds((A_BODY * it + g) * (GA * DA), GA * DA)]
                                     .rearrange("p t (h d) -> p t h d", h=GA)).then_inc(v4_ready, 1)
            for k in range(KC):
                pool.wait_ge(wo_in[k], 16)
                pool.tensor_copy(wo_h[:, k, :], wo_raw[:, k % 2, :]).then_inc(wo_high, 1)
                pool.wait_ge(wo_high, k + 1)
                pool.tensor_tensor(wo_l[:, k, :], wo_raw[:, k % 2, :], wo_h[:, k, :].bitcast(F32),
                                   ALU.subtract).then_inc(wo_low, 1)

        @block.tensor
        def _(pe):
            def piece(it, g, n, banks=PIECE_BANKS):
                hh, i, c, (k0, k1) = PIECES[n]
                b = g % A_BODY
                first_group = isinstance(it, int) and g == 0
                if n == 0 and first_group:
                    pe.wait_ge(half_loaded, 16 * 12)
                elif n == (NP // 2 if first_group else 0):
                    pe.wait_ge(loaded[b], 16 * 12 * (it + 1 + g // A_BODY))
                pe.wait_ge(piece_max, count(NP, it, g, n + 1 - len(banks)) if n >= len(banks) or g else 1)
                if n == 0:
                    pe.wait_ge(max_out, count(1, it, g, 0))
                out = ps[:, banks[n % len(banks)], 0:k1 - k0]
                last_span = k1 == P * (i + 1)
                last = pe.matmul(out, q_st[b][0:A_ROWS, hh, i * P:(i + 1) * P], k_st[b][0:A_ROWS, hh, k0:k1],
                                 start=True, stop=not last_span)
                if last_span:
                    last = pe.matmul(out[:, k1 - k0 - P:k1 - k0], const["ident_bf"][:, :], mask[:, :],
                                     start=False, stop=True)
                last.then_inc(piece_scored, 1)

            def turn_max(it, g):
                pe.wait_ge(link, count(LINKS, it, g, LINKS))
                pe.transpose(ps[0:A_PARTS * UNITS, 4, 0:P // 2].bitcast(BF16), max_part[:, :, :].rearrange("p a u -> p (a u)"),
                             const["ident_bf"][:, :]).then_inc(max_turned, 1)

            def score(it, tau):
                g, t = tau // S, tau % S
                k, h = A_STEPS[t]
                kind, half, _ = A_SETS[k]
                if t == 0:
                    pe.wait_ge(max_in[g], 16 * A_PARTS * (it + 1))
                pe.wait_ge(exped, 1 + A_BODY * S * it + max(0, tau - 1))
                for m in range(2 if kind == "rest" else 1):
                    for j, q0, col in blocks_a(k):
                        n = W - q0
                        own_keys = kind != "full"
                        bank, col = 2 * (t % 2) + (m if kind == "rest" else col // W), col % W
                        out = ps[:, bank, col:col + n]
                        last = pe.matmul(out, k_st[g][0:ROWS, h + m, j * P:(j + 1) * P],
                                         q_st[g][0:ROWS, h + m, half * W + q0:(half + 1) * W],
                                         start=True, stop=not own_keys)
                        if own_keys:
                            last = pe.matmul(out[:, 0:P], mask[:, :], const["ident_bf"][:, :], start=False, stop=True)
                last.then_inc(scored, 1)

            def mix(it, g, k, n):
                kind, half, _ = A_SETS[k]
                j, q0, col = blocks_a(k)[n]
                if n == 0:
                    pe.wait_ge(exped, count(S, it, g, A_SET_END[k] + 1))
                if j == 0:
                    pe.wait_ge(heads_out, count(2, it, g, half))
                if k == 0 and n == 0:
                    pe.wait_ge(v4_ready, count(1, it, g, 1))
                for hh in range(GA):
                    last = pe.matmul(ps[32 * hh:32 * hh + 32, 6, q0:W], v4[g % 2][:, j, hh, :],
                                     pt[:, k % 3, hh, col:col + W - q0], start=j == 0, stop=kind == "rest")
                if n == len(blocks_a(k)) - 1:
                    last.then_inc(mixed, 1)

            def turn_rows(it, g, half):
                job = 2 * g + half
                pe.wait_ge(rows_out, count(2, it, g, half + 1))
                for t in range(4):
                    last = pe.transpose(ps[:, 6, t * P:(t + 1) * P], o_rows[:, job % 2, t * P:(t + 1) * P],
                                        const["ident"][:, :])
                last.then_inc(rows_turned, 1)

            pe.wait_ge(made, 2)
            pe.wait_ge(v4_zeroed, 4)
            for n in range(NP):
                piece(0, 0, n, FIRST_BANKS)
            turn_max(0, 0)
            for n in range(pieces_before(SHIFT)):
                piece(0, 1, n, PIECE_BANKS)
            pe.wait_ge(ones_made, A_BODY)
            with pe.Fori(0, NGA // A_BODY) as it:
                for tau in range(A_BODY * S + 3):
                    g, t = tau // S, tau % S
                    if g < A_BODY:
                        score(it, tau)
                    for gg in range(A_BODY):
                        for k in range(SETS):
                            n = tau - (S * gg + A_SET_END[k] + 2)
                            if 0 <= n < len(blocks_a(k)):
                                mix(it, gg, k, n)
                    if g < A_BODY:
                        g, t = (tau + SHIFT) // S, (tau + SHIFT) % S
                        for n in range(pieces_before(t), pieces_before(t + 1)):
                            piece(it, g + 1, n)
                        if t == MAX_AT:
                            turn_max(it, g + 1)
                    for gg, half in jobs_at(tau, 1):
                        turn_rows(it, gg, half)

        @block.scalar
        def _(act):
            with act.Fori(0, NGA // A_BODY) as it:
                for tau in range(A_BODY * S + 3):
                    g, t = tau // S, tau % S
                    if g < A_BODY:
                        k, h = A_STEPS[t]
                        act.wait_ge(scored, count(S, it, g, t + 1))
                        act.wait_ge(mixed, 1 + A_BODY * SETS * it + max(0, SETS * g + k - 2))
                        pair = ps[:, 2 * (t % 2):2 * (t % 2) + 2, :]
                        if A_SETS[k][0] == "rest":
                            act.activation(pt[:, k % 3, h:h + 2, 0:W // 2], pair[:, :, 0:W // 2], ACT.Exp).then_inc(exped, 1)
                        else:
                            act.activation(pt[:, k % 3, h, :], pair.rearrange("p a b -> p (a b)"), ACT.Exp).then_inc(exped, 1)
                    for gg, half in jobs_at(tau, 0):
                        act.wait_ge(mixed, count(SETS, it, gg, 2 if half == 0 else SETS))
                        act.copy(o_rows[:, half, :], ps[:, 6, :]).then_inc(rows_out, 1)

        @block.vector
        def _(dve):
            def max_of_piece(it, g, n, banks=PIECE_BANKS):
                hh, i, c, (k0, k1) = PIECES[n]
                u = hh * NT + i
                dve.wait_ge(piece_scored, count(NP, it, g, n + 1))
                dve.tensor_reduce(part_max[:, c, u:u + 1], ps[:, banks[n % len(banks)], 0:k1 - k0], AX.X, ALU.max).then_inc(piece_max, 1)

            def split_max(it, g):
                dve.wait_ge(piece_max, count(NP, it, g, NP))
                dve.tensor_tensor(row_max[:, :], part_max[:, 0, :], part_max[:, 1, :], ALU.max).then_inc(link, 1)
                dve.wait_ge(link, count(LINKS, it, g, 1))
                dve.tensor_scalar(max_part[:, 0, :], row_max[:, :], -1.0, None, ALU.mult).then_inc(link, 1)
                dve.wait_ge(link, count(LINKS, it, g, 2))
                dve.scalar_tensor_tensor(max_rest[:, :], row_max[:, :], -1.0, max_part[:, 0, :],
                                         ALU.mult, ALU.subtract).then_inc(link, 1)
                dve.wait_ge(link, count(LINKS, it, g, 3))
                dve.tensor_copy(max_part[:, 1, :], max_rest[:, :]).then_inc(link, 1)
                dve.wait_ge(link, count(LINKS, it, g, 4))
                dve.tensor_tensor(max_part[:, 2, :], max_rest[:, :], max_part[:, 1, :], ALU.subtract).then_inc(link, 1)

            def take_max(it, g):
                dve.wait_ge(max_turned, count(1, it, g, 1))
                if g:
                    dve.wait_ge(max_in[g - 1], 16 * A_PARTS * (it + 1))
                dve.tensor_copy(max_rows[0:A_PARTS * UNITS, :], ps[0:A_PARTS * UNITS, 4, 0:P // 2].bitcast(BF16)
                                ).then_inc(max_out, 1)

            dve.memset(part_max[:, 1, :], -3e38).then_inc(made, 1)
            dve.tensor_scalar(mask[:, :], const["rel"][:, SLIDE:SLIDE + P], 0.5 * NEG, NEG, ALU.is_le, ALU.mult).then_inc(made, 1)
            dve.wait_ge(made, 2)
            for n in range(NP):
                max_of_piece(0, 0, n, FIRST_BANKS)
            split_max(0, 0)
            take_max(0, 0)
            for n in range(pieces_before(SHIFT)):
                max_of_piece(0, 1, n, PIECE_BANKS)
            with dve.Fori(0, NGA // A_BODY) as it:
                for tau in range(A_BODY * S + 3):
                    g, t = tau // S, tau % S
                    if g < A_BODY:
                        g, t = (tau + SHIFT) // S, (tau + SHIFT) % S
                        for n in range(pieces_before(t), pieces_before(t + 1)):
                            max_of_piece(it, g + 1, n)
                        if t == SPLIT_AT:
                            split_max(it, g + 1)
                        if t == MAX_AT:
                            take_max(it, g + 1)
                    for gg, half in jobs_at(tau, 1):
                        dve.wait_ge(rows_turned, count(2, it, gg, half + 1))
                        tok = ps[:, 6, :].rearrange("p (t h d) -> p t h d", t=4, h=GA)
                        dve.reciprocal(recip[:, :, :], tok[:, :, :, DA]).then_inc(recip_done, 1)
                        dve.wait_ge(recip_done, count(2, it, gg, half + 1))
                        dst = o_all[:, 4 * half:4 * half + 4, bass.ds((A_BODY * it + gg) * (GA * DA), GA * DA)]
                        dve.tensor_tensor(dst.rearrange("p t (h d) -> p t h d", h=GA), tok[:, :, :, 0:DA],
                                          recip[:, :, :].unsqueeze(3).to_broadcast([P, 4, GA, DA]),
                                          ALU.mult).then_inc(heads_out, 1)


def rotary_output_block(nc, ctx, x, o_all, w_h, w_l, stats, const, ps):
    def sem(name):
        return ctx.enter_context(nc.semaphore(f"ro_{name}"))

    with ExitStack() as own:
        def sb(name, shape, dt=F32):
            return own.enter_context(nc.sbuf_tensor(f"ro_{name}", shape, dt))

        ot_h = sb("ot_h", [P, KC, T], F32R)
        ot_l = sb("ot_l", [P, KC, T], F32R)
        turned = sem("turned")
        high_done = sem("high_done")
        low_done = sem("low_done")
        projected = sem("projected")
        added = sem("added")
        block = own.enter_context(nc.Block())

        @block.tensor
        def _(pe):
            for i in range(NT + 1):
                if i < NT:
                    if i >= 2:
                        pe.wait_ge(low_done, i - 1)
                    for k in range(KC):
                        last = pe.transpose(ps[:, 4 + i % 2, k * P:(k + 1) * P], o_all[:, i, k * P:(k + 1) * P],
                                            const["ident"][:, :])
                    last.then_inc(turned, 1)
                if i >= 1:
                    j = i - 1
                    pe.wait_ge(low_done, j + 1)
                    if j >= 2:
                        pe.wait_ge(added, j - 1)
                    for k in range(KC):
                        last = three_pass(pe, ps[:, j % 2, :], (ot_h[:, k, j * P:(j + 1) * P], ot_l[:, k, j * P:(j + 1) * P]),
                                          (w_h[:, k, :], w_l[:, k, :]), k == 0, k == KC - 1)
                    last.then_inc(projected, 1)

        @block.scalar
        def _(act):
            for i in range(NT):
                act.wait_ge(turned, i + 1)
                act.copy(ot_h[:, :, i * P:(i + 1) * P],
                         ps[:, 4 + i % 2, :].rearrange("p (k t) -> p k t", k=KC)).then_inc(high_done, 1)

        @block.vector
        def _(dve):
            for i in range(NT + 1):
                if i < NT:
                    dve.wait_ge(high_done, i + 1)
                    dve.tensor_tensor(ot_l[:, :, i * P:(i + 1) * P],
                                      ps[:, 4 + i % 2, :].rearrange("p (k t) -> p k t", k=KC),
                                      ot_h[:, :, i * P:(i + 1) * P].bitcast(F32), ALU.subtract).then_inc(low_done, 1)
                if i >= 1:
                    j = i - 1
                    dve.wait_ge(projected, j + 1)
                    dve.tensor_tensor(x[:, j, :], ps[:, j % 2, :], x[:, j, :], ALU.add).then_inc(added, 1)
                    if j >= 1:
                        dve.wait_ge(added, j)
                        take_stats(dve, stats, x, j - 1)
            dve.wait_ge(added, NT)
            take_stats(dve, stats, x, NT - 1)


def ffn_block(nc, ctx, tag, norm, x, xt_h, xt_l, w_h, w_l, wb_h, wb_l, const, ps, bias_dram, stats=None, out_dram=None):
    def sem(name):
        return ctx.enter_context(nc.semaphore(f"{tag}_{name}"))

    N = C + ER + NE
    NA = ER + NE
    NH = 256
    with ExitStack() as own:
        def sb(name, shape, dt=F32):
            return own.enter_context(nc.sbuf_tensor(f"{tag}_{name}", shape, dt))

        bias = sb("bias", [P, C])
        hid = sb("hid", [P, NT, NA])
        top = sb("top", [P, NT, 8])
        top_i = sb("top_i", [P, NT, 8], U32)
        top_f = sb("top_f", [P, NT, 2])
        gap = sb("gap", [P, NT])
        gap_e = sb("gap_e", [P, NT])
        gap_s = sb("gap_s", [P, NT])
        w_top = sb("w_top", [P, NT, 2])
        sel = sb("sel", [P, 2, NT, NE])
        w_e = sb("w_e", [P, NT, NE])
        hw = sb("hw", [P, NT, ER])
        ht_h = sb("ht_h", [P, 2, P], F32R)
        ht_l = sb("ht_l", [P, 2, P], F32R)
        b_in = sem("b_in")
        hidden = sem("hidden")
        hid_out = sem("hid_out")
        step = sem("step")
        exp_done = sem("exp_done")
        gated = sem("gated")
        turned = sem("turned")
        ht_high = sem("ht_high")
        ht_low = sem("ht_low")
        summed = sem("summed")
        biased = sem("biased")
        added = sem("added")
        stored = sem("stored")
        block = own.enter_context(nc.Block())

        @block.sync
        def _(sp):
            norm.load_weights(sp)
            sp.dma_start(bias[:, :], bias_dram.partition_broadcast(P)).then_inc(b_in, 16)
            if out_dram is not None:
                for i in range(NT):
                    sp.wait_ge(added, i + 1)
                    sp.dma_start(out_dram[i * P:(i + 1) * P, :], x[:, i, :]).then_inc(stored, 16)
                sp.wait_ge(stored, 16 * NT)

        @block.gpsimd
        def _(pool):
            norm.on_pool(pool)

        @block.tensor
        def _(pe):
            def cols(i):
                return slice(i * P, (i + 1) * P)

            norm.turn(pe, 0)
            for i in range(NT):
                if i + 1 < NT:
                    norm.turn(pe, i + 1)
                pe.wait_ge(norm.low_done, i + 1)
                if i >= 4:
                    pe.wait_ge(hid_out, i - 3)
                for k in range(KC):
                    if i == 0:
                        pe.wait_ge(norm.w_low, k + 1)
                    last = three_pass(pe, ps[:, i % 4, 0:NH], (xt_h[:, k, cols(i)], xt_l[:, k, cols(i)]),
                                      (w_h[:, k, N - NH:N], w_l[:, k, N - NH:N]), k == 0, k == KC - 1)
                last.then_inc(hidden, 1)
            for s in range(NT + 2):
                if s < NT:
                    if s < 4:
                        pe.wait_ge(hid_out, NT - 3 + s)
                    else:
                        pe.wait_ge(added, s - 3)
                    for k in range(KC):
                        three_pass(pe, ps[:, s % 4, :], (xt_h[:, k, cols(s)], xt_l[:, k, cols(s)]),
                                   (w_h[:, k, 0:C], w_l[:, k, 0:C]), k == 0, False)
                if 1 <= s <= NT:
                    i = s - 1
                    pe.wait_ge(gated, i + 1)
                    if i >= 2:
                        pe.wait_ge(ht_low, i - 1)
                    pe.transpose(ps[:, 6 + i % 2, 0:P], hw[:, i, :], const["ident"][:, :]).then_inc(turned, 1)
                if s >= 2:
                    j = s - 2
                    pe.wait_ge(ht_low, j + 1)
                    if j == 0:
                        pe.wait_ge(norm.w_low, KC + 1)
                    three_pass(pe, ps[:, j % 4, :], (ht_h[:, j % 2, :], ht_l[:, j % 2, :]),
                               (wb_h[:, 0, :], wb_l[:, 0, :]), False, True).then_inc(summed, 1)

        @block.scalar
        def _(act):
            norm.split_weights(act, 0, 1)
            norm.take(act, 0)
            norm.split_weights(act, 1, 2)
            norm.take(act, 1)
            norm.split_weights(act, 2)
            for i in range(NT):
                if 2 <= i + 1 < NT:
                    norm.take(act, i + 1)
                act.wait_ge(hidden, i + 1)
                act.copy(hid[:, i, :], ps[:, i % 4, NH - NA:NH]).then_inc(hid_out, 1)
            act.wait_ge(step, 1 + 2 * NT)
            act.activation(gap_e[:, :], gap[:, :], ACT.Exp).then_inc(exp_done, 1)
            for i in range(NT):
                act.wait_ge(turned, i + 1)
                if i >= 2:
                    act.wait_ge(summed, i - 1)
                act.copy(ht_h[:, i % 2, :], ps[:, 6 + i % 2, 0:P]).then_inc(ht_high, 1)

        @block.vector
        def _(dve):
            done = [0]

            def link(ins):
                done[0] += 1
                ins.then_inc(step, 1)
                dve.wait_ge(step, done[0])

            norm.on_vector(dve)
            for i in range(NT):
                dve.wait_ge(hid_out, i + 1)
                link(dve.max(top[:, i, :], hid[:, i, ER:NA]))
                link(dve.max_index(top_i[:, i, :], top[:, i, :], hid[:, i, ER:NA]))
            link(dve.tensor_tensor(gap[:, :], top[:, :, 1], top[:, :, 0], ALU.subtract))
            link(dve.tensor_copy(top_f[:, :, :], top_i[:, :, 0:2]))
            dve.wait_ge(exp_done, 1)
            link(dve.tensor_scalar(gap_s[:, :], gap_e[:, :], 1.0 / SCALING, 1.0 / SCALING, ALU.mult, ALU.add))
            link(dve.reciprocal(w_top[:, :, 0], gap_s[:, :]))
            link(dve.tensor_tensor(w_top[:, :, 1], gap_e[:, :], w_top[:, :, 0], ALU.mult))
            for r in range(2):
                link(dve.tensor_tensor(sel[:, r, :, :], const["iota"][:, :].unsqueeze(1).to_broadcast([P, NT, NE]),
                                       top_f[:, :, r].unsqueeze(2).to_broadcast([P, NT, NE]), ALU.is_equal))
                link(dve.tensor_tensor(sel[:, r, :, :], sel[:, r, :, :],
                                       w_top[:, :, r].unsqueeze(2).to_broadcast([P, NT, NE]), ALU.mult))
            link(dve.tensor_tensor(w_e[:, :, :], sel[:, 0, :, :], sel[:, 1, :, :], ALU.add))
            for i in range(NT):
                dve.tensor_tensor(hw[:, i, :].rearrange("p (e r) -> p e r", e=NE),
                                  hid[:, i, 0:ER].rearrange("p (e r) -> p e r", e=NE),
                                  w_e[:, i, :].unsqueeze(2).to_broadcast([P, NE, NR]), ALU.mult).then_inc(gated, 1)
            dve.wait_ge(b_in, 16)
            for i in range(NT + 1):
                if i < NT:
                    dve.tensor_tensor(x[:, i, :], x[:, i, :], bias[:, :], ALU.add).then_inc(biased, 1)
                    dve.wait_ge(ht_high, i + 1)
                    dve.tensor_tensor(ht_l[:, i % 2, :], ps[:, 6 + i % 2, 0:P], ht_h[:, i % 2, :].bitcast(F32),
                                      ALU.subtract).then_inc(ht_low, 1)
                if i >= 1:
                    j = i - 1
                    dve.wait_ge(summed, j + 1)
                    dve.wait_ge(biased, j + 1)
                    dve.tensor_tensor(x[:, j, :], ps[:, j % 4, :], x[:, j, :], ALU.add).then_inc(added, 1)
                    if stats and j >= 1:
                        dve.wait_ge(added, j)
                        take_stats(dve, stats, x, j - 1)
            if stats:
                dve.wait_ge(added, NT)
                take_stats(dve, stats, x, NT - 1)


def alibi_attention_block(nc, ctx, x, xt_h, xt_l, w_h, w_l, credited, const, ps, wqkv_dram, wo_dram):
    def sem(name):
        return credited[name] if name in credited else ctx.enter_context(nc.semaphore(f"ab_{name}"))

    U = GB * NT
    NG = groups_before_b(U)
    JOBS = U // 2
    PAIR = 2 * P
    WEIGHT_JOBS = 12
    NQ = GB * DB
    NW = NQ + 2 * DB
    with ExitStack() as own:
        def sb(name, shape, dt=F32):
            return own.enter_context(nc.sbuf_tensor(f"ab_{name}", shape, dt))

        raw = sb("raw", [P, 2, NW])
        wo_h = sb("wo_h", [P, GB, C], F32R)
        wo_l = sb("wo_l", [P, GB, C], F32R)
        qt_h = sb("qt_h", [P, GB, T], F32R)
        qt_l = sb("qt_l", [P, GB, T], F32R)
        kt_h = sb("kt_h", [P, T], F32R)
        kt_l = sb("kt_l", [P, T], F32R)
        v_h = sb("v_h", [P, NT, DB], F32R)
        v_l = sb("v_l", [P, NT, DB], F32R)
        nat = sb("nat", [P, 2, GB + 1, DB])
        squares = sb("squares", [P, GB + 1, DB], BF16)
        sq_sum = sb("sq_sum", [P, NT, GB + 1])
        ms_eps = sb("ms_eps", [P, NT, GB + 1])
        rms = sb("rms", [P, NT, GB + 1])
        prob = sb("prob", [P, 3, T])
        pt_h = sb("pt_h", [P, 2, NT, PAIR], F32R)
        pt_l = sb("pt_l", [P, 2, NT, PAIR], F32R)
        o_raw = sb("o_raw", [P, 2, PAIR])
        bias = sb("bias", [P, T])
        neg_max = sb("neg_max", [P, U])
        sums = sb("sums", [P, U])
        recip = sb("recip", [P, U])
        gate = sb("gate", [P, U])
        gate_pool = sb("gate_pool", [P, GB + KC + JOBS])
        raw_in = [sem(f"raw_in{b}") for b in range(2)]
        split = sem("split")
        split_high = sem("split_high")
        split_o = sem("split_o")
        projected = sem("projected")
        squared = sem("squared")
        ms_ready = sem("ms_ready")
        rms_ready = sem("rms_ready")
        v_high = sem("v_high")
        scaled = sem("scaled")
        qk_turned = sem("qk_turned")
        qk_high = sem("qk_high")
        qk_low = sem("qk_low")
        bias_ready = sem("bias_ready")
        scored = sem("scored")
        shifted = sem("shifted")
        exped = sem("exped")
        recip_done = sem("recip_done")
        turned = sem("turned")
        zeroed = sem("zeroed")
        pt_high = sem("pt_high")
        pt_low = sem("pt_low")
        mixed = sem("mixed")
        o_out = sem("o_out")
        o_high = sem("o_high")
        o_low = sem("o_low")
        out_done = sem("out_done")
        added = sem("added")
        block = own.enter_context(nc.Block())

        def place(pair, j):
            return j + NT - 2 - 2 * pair

        OUTS = [(2 * pair + t, h) for pair in range(NT // 2 - 1) for h in range(GB) for t in range(2)]
        EARLY = len(OUTS)
        OUTS += [(i, h) for i in (NT - 2, NT - 1) for h in range(GB)]
        NO = len(OUTS)

        def out_bank(n):
            return n % 4 if n < EARLY else 6 + n % 2

        def outs_of(i):
            return [n for n, (t, _) in enumerate(OUTS) if t == i]

        def finished(s):
            return (s - 5) // 2 if s >= 5 and s % 2 == 1 else None

        @block.sync
        def _(sp):
            def load_qkv(g, k):
                sp.dma_start(raw[:, k % 2, :], wqkv_dram[bass.ds(g, 1), k * P:(k + 1) * P, :].squeeze(0)
                             ).then_inc(raw_in[k % 2], 16)

            def load_wo(g, k):
                if k < 2:
                    sp.wait_ge(split, 1 + KC * g)
                else:
                    sp.wait_ge(split_o, 1 + GB * g + k - 1)
                sp.dma_start(raw[:, k % 2, 0:C], wo_dram[bass.ds(g, 1), k * P:(k + 1) * P, :].squeeze(0)
                             ).then_inc(raw_in[k % 2], 16)

            with sp.Fori(0, KVB - 1) as g:
                for k in range(GB):
                    load_wo(g, k)
                for k in range(KC):
                    if k < 2:
                        sp.wait_ge(split_o, 1 + GB * g + GB - 1 + k)
                    else:
                        sp.wait_ge(split, 1 + KC * g + k - 1)
                    load_qkv(g + 1, k)
            for k in range(GB):
                load_wo(KVB - 1, k)

        @block.gpsimd
        def _(pool):
            def carry_wait(n):
                pool.tensor_tensor(gate_pool[:, n:n + 1], const["neg_half"][:, 0:1], const["neg_half"][:, 0:1], ALU.add)

            def powers(g):
                for i in range(NT):
                    pool.wait_ge(ms_ready, 1 + NT * g + i + 1)
                    pool.tensor_tensor(rms[:, i, :], ms_eps[:, i, :], const["neg_half"][:, 0:GB + 1], ALU.pow).then_inc(rms_ready, 1)

            def split_step(g, last):
                def half_piece(m):
                    k = m // 2 % KC
                    buf = raw[:, k % 2, 0:C] if m < 8 else raw[:, k % 2, :]
                    high, low, done = (wo_h, wo_l, split_o) if m < 8 else (w_h, w_l, split)
                    if m == 0:
                        pool.wait_ge(out_done, 1 + NO * g)
                    if m == 8:
                        pool.wait_ge(projected, 1 + NT * g + NT)
                    if m % 2 == 0:
                        pool.wait_ge(raw_in[k % 2], 64 * g + 32 * (m // 8) + 16 * (k // 2 + 1))
                        carry_wait(m // 2)
                        pool.tensor_copy(high[:, k, :], buf).then_inc(split_high, 1)
                    else:
                        pool.wait_ge(split_high, 1 + 8 * g + m // 2 + 1)
                        pool.tensor_tensor(low[:, k, :], buf, high[:, k, :].bitcast(F32), ALU.subtract).then_inc(done, 1)

                for n in range(JOBS):
                    for m in range(16 * n // WEIGHT_JOBS, 16 * (n + 1) // WEIGHT_JOBS):
                        if m < 8 or (m < 16 and not last):
                            half_piece(m)
                    pair = slice(n % 4 * PAIR, (n % 4 + 1) * PAIR)
                    pool.wait_ge(o_out, 1 + JOBS * g + n + 1)
                    carry_wait(GB + KC + n)
                    pool.tensor_copy(qt_h[:, n // 4, pair], o_raw[:, n % 2, :]).then_inc(o_high, 1)
                    pool.wait_ge(o_high, 1 + JOBS * g + n + 1)
                    pool.tensor_tensor(qt_l[:, n // 4, pair], o_raw[:, n % 2, :], qt_h[:, n // 4, pair].bitcast(F32),
                                       ALU.subtract).then_inc(o_low, 1)

            powers(0)
            with pool.Fori(0, KVB - 1) as g:
                split_step(g, False)
                powers(g + 1)
            split_step(KVB - 1, True)

        @block.tensor
        def _(pe):
            pe.wait_ge(zeroed, 2)
            def project(g, i, first):
                if i == 0:
                    pe.wait_ge(split, 1 + KC * g)
                if i < 2 and not first:
                    pe.wait_ge(added, 1 + NO * g - (NO - EARLY) - 2 + 2 * i)
                if i >= 2:
                    pe.wait_ge(scaled, 1 + NT * g + i - 1)
                cols = slice(i * P, (i + 1) * P)
                b0 = 2 * (i % 2)
                for k in range(KC):
                    three_pass(pe, ps[:, b0, :], (xt_h[:, k, cols], xt_l[:, k, cols]),
                               (w_h[:, k, 0:NQ], w_l[:, k, 0:NQ]), k == 0, k == KC - 1)
                    last = three_pass(pe, ps[:, b0 + 1, 0:2 * DB], (xt_h[:, k, cols], xt_l[:, k, cols]),
                                      (w_h[:, k, NQ:NW], w_l[:, k, NQ:NW]), k == 0, k == KC - 1)
                last.then_inc(projected, 1)

            def turn_qk(g, i):
                pe.wait_ge(scaled, 1 + NT * g + i + 1)
                if i == 0:
                    pe.wait_ge(pt_low, 1 + NG * g)
                else:
                    pe.wait_ge(qk_low, 1 + NT * g + i)
                for h in range(GB + 1):
                    at = h * P if h < GB else 0
                    last = pe.transpose(ps[:, 4 + h // GB, at:at + P], nat[:, i % 2, h, :], const["ident"][:, :])
                last.then_inc(qk_turned, 1)

            def score(g, v):
                hh, i = v // NT, v % NT
                if v < NT:
                    pe.wait_ge(qk_low, 1 + NT * g + (i | 1) + 1)
                if v >= 2:
                    pe.wait_ge(shifted, 1 + U * g + v - 1)
                for c, (k0, k1) in enumerate(key_spans(i)):
                    k1 = max(k1, k0 + PAIR)
                    last = three_pass(pe, ps[:, 2 * (v % 2) + c, 0:k1 - k0],
                                      (qt_h[:, hh, i * P:(i + 1) * P], qt_l[:, hh, i * P:(i + 1) * P]),
                                      (kt_h[:, k0:k1], kt_l[:, k0:k1]), True, True)
                last.then_inc(scored, 1)

            def turn(g, v):
                pe.wait_ge(exped, 1 + U * g + v + 1)
                for k, (j0, nb) in enumerate(key_groups(v % NT)):
                    n = groups_before_b(v) + k
                    if n >= 3:
                        pe.wait_ge(pt_low, 1 + NG * g + n - 2)
                    for j in range(nb):
                        last = pe.transpose(ps[:, 4 + n % 3, j * P:(j + 1) * P],
                                            prob[:, v % 3, (j0 + j) * P:(j0 + j + 1) * P], const["ident"][:, :])
                    last.then_inc(turned, 1)

            def mix(g, job, part):
                pair = job % 4
                if part == 0:
                    pe.wait_ge(pt_low, 1 + NG * g + groups_before_b(2 * job + 2))
                    if job == 0:
                        pe.wait_ge(added, 1 + NO * g)
                    else:
                        pe.wait_ge(o_out, 1 + JOBS * g + job)
                for j in range(part * (pair + 1), (part + 1) * (pair + 1)):
                    at = place(pair, j)
                    last = three_pass(pe, ps[:, 7, 0:PAIR], (v_h[:, j, :], v_l[:, j, :]),
                                      (pt_h[:, job % 2, at, :], pt_l[:, job % 2, at, :]),
                                      j == 0, j == 2 * pair + 1)
                if part == 1:
                    last.then_inc(mixed, 1)

            def project_out(g, n):
                i, h = OUTS[n]
                if n == 0:
                    pe.wait_ge(split_o, 1 + GB * g + GB)
                if h == 0 and i % 2 == 0:
                    pe.wait_ge(o_low, 1 + JOBS * g + JOBS - 3 + i // 2)
                if n in (0, 2):
                    pe.wait_ge(shifted, 1 + U * g + U - 1 + n // 2)
                elif 4 <= n < EARLY:
                    pe.wait_ge(added, 1 + NO * g + n - 3)
                elif n >= EARLY + 2:
                    pe.wait_ge(added, 1 + NO * g + n - 1)
                three_pass(pe, ps[:, out_bank(n), :],
                           (qt_h[:, h, i * P:(i + 1) * P], qt_l[:, h, i * P:(i + 1) * P]),
                           (wo_h[:, h, :], wo_l[:, h, :]), True, True).then_inc(out_done, 1)

            def projections(g, first):
                for i in range(NT + 1):
                    if i < NT:
                        project(g, i, first)
                    if i >= 1:
                        if i >= NT - 1 and not first:
                            for n in outs_of(i - 1):
                                project_out(g - 1, n)
                        turn_qk(g, i - 1)

            def attention(g):
                for s in range(U + 4):
                    if s < U:
                        score(g, s)
                    if 0 <= s - 2 < U:
                        turn(g, s - 2)
                    if s >= 4:
                        mix(g, (s - 4) // 2, s % 2)
                    if s >= U:
                        for n in range(4 * (s - U), 4 * (s - U + 1)):
                            project_out(g, n)

            projections(0, True)
            with pe.Fori(0, KVB - 1) as g:
                attention(g)
                for n in range(16, EARLY):
                    project_out(g, n)
                projections(g + 1, False)
            attention(KVB - 1)
            for n in range(16, NO):
                project_out(KVB - 1, n)

        @block.scalar
        def _(act):
            def squares_of(g, i):
                b0 = 2 * (i % 2)
                act.wait_ge(projected, 1 + NT * g + i + 1)
                act.wait_ge(squared, 1 + NT * g + i)
                for h in range(GB + 1):
                    src = ps[:, b0, h * P:(h + 1) * P] if h < GB else ps[:, b0 + 1, 0:DB]
                    last = act.activation(squares[:, h, :], src, ACT.Square, accum_out=sq_sum[:, i, h:h + 1])
                last.then_inc(squared, 1)
                act.copy(v_h[:, i, :], ps[:, b0 + 1, DB:2 * DB]).then_inc(v_high, 1)

            def take_qk(g, i):
                act.wait_ge(qk_turned, 1 + NT * g + i + 1)
                act.copy(qt_h[:, :, i * P:(i + 1) * P], ps[:, 4, :].rearrange("p (h t) -> p h t", h=GB))
                act.copy(kt_h[:, i * P:(i + 1) * P], ps[:, 5, 0:P]).then_inc(qk_high, 1)

            def projections(g):
                for i in range(NT + 1):
                    if i < NT:
                        squares_of(g, i)
                    if i >= 1:
                        take_qk(g, i - 1)

            def attention(g):
                for s in range(U + 4):
                    if 0 <= s - 2 < U:
                        v = s - 2
                        job, col = v // 2, (v % 2) * P
                        for k, (j0, nb) in enumerate(key_groups(v % NT)):
                            n = groups_before_b(v) + k
                            act.wait_ge(turned, 1 + NG * g + n + 1)
                            act.wait_ge(mixed, 1 + JOBS * g + max(0, job - 1))
                            s0 = place(job % 4, j0)
                            act.copy(pt_h[:, job % 2, s0:s0 + nb, col:col + P],
                                     ps[:, 4 + n % 3, 0:nb * P].rearrange("p (j q) -> p j q", q=P)).then_inc(pt_high, 1)
                    if s < U:
                        w = P * (s % NT + 1)
                        act.wait_ge(shifted, 1 + U * g + s + 1)
                        act.activation(prob[:, s % 3, 0:w], prob[:, s % 3, 0:w], ACT.Exp, bias=neg_max[:, s:s + 1],
                                       scale=-1.0, accum_out=sums[:, s:s + 1]).then_inc(exped, 1)
                    job = finished(s)
                    if job is not None:
                        act.wait_ge(mixed, 1 + JOBS * g + job + 1)
                        act.wait_ge(o_low, 1 + JOBS * g + max(0, job - 1))
                        act.copy(o_raw[:, job % 2, :], ps[:, 7, 0:PAIR]).then_inc(o_out, 1)

            projections(0)
            with act.Fori(0, KVB - 1) as g:
                attention(g)
                projections(g + 1)
            attention(KVB - 1)

        @block.vector
        def _(dve):
            for part in (pt_h, pt_l):
                dve.tensor_scalar(part[:, :, NT - 1, 0:P], const["rel"][:, 0:2 * P].rearrange("p (b q) -> p b q", b=2),
                                  0.0, None, ALU.mult).then_inc(zeroed, 1)
            def take_qk_low(g, i):
                dve.wait_ge(qk_high, 1 + NT * g + i + 1)
                cols = slice(i * P, (i + 1) * P)
                dve.tensor_tensor(qt_l[:, :, cols], ps[:, 4, :].rearrange("p (h t) -> p h t", h=GB),
                                  qt_h[:, :, cols].bitcast(F32), ALU.subtract)
                dve.tensor_tensor(kt_l[:, cols], ps[:, 5, 0:P], kt_h[:, cols].bitcast(F32), ALU.subtract).then_inc(qk_low, 1)

            def add_out(g, n):
                i, h = OUTS[n]
                dve.wait_ge(added, 1 + NO * g + (n if n > EARLY else max(0, n - 1)))
                dve.wait_ge(out_done, 1 + NO * g + n + 1)
                u = h * NT + i
                dve.scalar_tensor_tensor(x[:, i, :], ps[:, out_bank(n), :], recip[:, u:u + 1], x[:, i, :],
                                         ALU.mult, ALU.add).then_inc(added, 1)

            def scale_qk(g, i):
                b0 = 2 * (i % 2)
                dve.wait_ge(rms_ready, 1 + NT * g + i + 1)
                dve.wait_ge(v_high, 1 + NT * g + i + 1)
                dve.tensor_tensor(nat[:, i % 2, 0:GB, :], ps[:, b0, :].rearrange("p (h d) -> p h d", h=GB),
                                  rms[:, i, 0:GB].unsqueeze(2).to_broadcast([P, GB, DB]), ALU.mult)
                dve.scalar_tensor_tensor(nat[:, i % 2, GB, :], ps[:, b0 + 1, 0:DB], rms[:, i, GB:GB + 1],
                                         const["w_norm"][:, :], ALU.mult, ALU.mult)
                dve.tensor_tensor(v_l[:, i, :], ps[:, b0 + 1, DB:2 * DB], v_h[:, i, :].bitcast(F32),
                                  ALU.subtract).then_inc(scaled, 1)

            def projections(g, first):
                for i in range(NT):
                    dve.wait_ge(squared, 1 + NT * g + i + 1)
                    dve.tensor_scalar(ms_eps[:, i, :], sq_sum[:, i, :], 1.0 / DB, RMS_EPS, ALU.mult, ALU.add).then_inc(ms_ready, 1)
                    if 1 <= i < NT - 1:
                        take_qk_low(g, i - 1)
                    if i == NT - 1 and not first:
                        for n in outs_of(NT - 2):
                            add_out(g - 1, n)
                    scale_qk(g, i)
                last = outs_of(NT - 1)
                if not first:
                    for n in last[:2]:
                        add_out(g - 1, n)
                take_qk_low(g, NT - 2)
                if not first:
                    for n in last[2:]:
                        add_out(g - 1, n)
                take_qk_low(g, NT - 1)

            def attention(g):
                for s in range(U + 4):
                    if s in (U, U + 3):
                        u0, u1 = (0, U - 4) if s == U else (U - 4, U)
                        dve.wait_ge(exped, 1 + U * g + u1)
                        dve.reciprocal(recip[:, u0:u1], sums[:, u0:u1]).then_inc(recip_done, 1)
                        dve.wait_ge(recip_done, 1 + 2 * g + (1 if s == U else 2))
                    if s < U:
                        i = s % NT
                        w = P * (i + 1)
                        if i == 0:
                            dve.wait_ge(shifted, 1 + U * g + s)
                            dve.tensor_scalar(bias[:, :], const["rel"][:, :], const["slopes"][:, bass.ds(g * GB + s // NT, 1)],
                                              None, ALU.mult).then_inc(bias_ready, 1)
                            dve.wait_ge(bias_ready, 1 + GB * g + s // NT + 1)
                        dve.wait_ge(scored, 1 + U * g + s + 1)
                        dve.wait_ge(turned, 1 + NG * g + (groups_before_b(s - 2) if s >= 3 else 0))
                        dve.memset(gate[:, s:s + 1], 0.0)
                        dve.tensor_tensor_reduce(out=prob[:, s % 3, 0:w],
                                                 in0=ps[:, 2 * (s % 2):2 * (s % 2) + 2, :].rearrange("p a b -> p (a b)")[:, 0:w],
                                                 in1=bias[:, SLIDE - i * P:T], scale=-1.0, scalar=3e38,
                                                 op0=ALU.add, op1=ALU.min,
                                                 accum_out=neg_max[:, s:s + 1]).then_inc(shifted, 1)
                    if 0 <= s - 2 < U:
                        v = s - 2
                        job, col = v // 2, (v % 2) * P
                        for k, (j0, nb) in enumerate(key_groups(v % NT)):
                            n = groups_before_b(v) + k
                            s0 = place(job % 4, j0)
                            dve.wait_ge(pt_high, 1 + NG * g + n + 1)
                            dve.tensor_tensor(pt_l[:, job % 2, s0:s0 + nb, col:col + P],
                                              ps[:, 4 + n % 3, 0:nb * P].rearrange("p (j q) -> p j q", q=P),
                                              pt_h[:, job % 2, s0:s0 + nb, col:col + P].bitcast(F32),
                                              ALU.subtract).then_inc(pt_low, 1)
                    if s >= U:
                        for n in range(4 * (s - U), 4 * (s - U + 1)):
                            add_out(g, n)

            projections(0, True)
            with dve.Fori(0, KVB - 1) as g:
                attention(g)
                for n in range(16, EARLY):
                    add_out(g, n)
                projections(g + 1, False)
            attention(KVB - 1)
            for n in range(16, NO):
                add_out(KVB - 1, n)


def hybrid_layer_kernel(nc, ins, out_dram):
    with ExitStack() as ctx:
        def sb(name, shape, dt=F32):
            return ctx.enter_context(nc.sbuf_tensor(name, shape, dt))

        x = sb("x", [P, NT, C])
        const = {
            "ident": sb("ident", [P, P]),
            "ident_bf": sb("ident_bf", [P, P], BF16),
            "rel": sb("rel", [P, T]),
            "trig": sb("trig", [P, NT, 4]),
            "slopes": sb("slopes", [P, HB]),
            "iota": sb("iota", [P, NE]),
            "neg_half": sb("neg_half", [P, NT]),
            "w_norm": sb("w_norm", [P, DB]),
        }
        w_norm2 = sb("w_norm2", [P, 2, DB])
        ps = ctx.enter_context(nc.psum_tensor("ps", [P, 8, W], F32))
        parts_dram = [nc.dram_tensor(f"parts{a}", [2 * (C + 2 * GA * DA), T], BF16, kind="Internal").ap() for a in range(3)]
        x_in = [ctx.enter_context(nc.semaphore(f"x_in{share}")) for share in range(4)]
        loaded = ctx.enter_context(nc.semaphore("const_loaded"))
        made = ctx.enter_context(nc.semaphore("const_made"))

        def with_xt(tag, w_drams, use, merged=True, **options):
            with ExitStack() as own:
                xt_h = own.enter_context(nc.sbuf_tensor(f"{tag}_xt_h", [P, KC, T], F32R))
                xt_l = own.enter_context(nc.sbuf_tensor(f"{tag}_xt_l", [P, KC, T], F32R))
                parts, pieces = [], []
                for m, dram in enumerate(w_drams):
                    rows, n = dram.shape
                    high, low = (own.enter_context(nc.sbuf_tensor(f"{tag}_w{m}_{part}", [P, rows // P, n], F32R))
                                 for part in "hl")
                    parts += [high, low]
                    pieces += [(dram[k * P:(k + 1) * P, :], high[:, k, :], low[:, k, :]) for k in range(rows // P)]
                if merged:
                    norm = LayerNorm(nc, ctx, own, f"{tag}n", x, xt_h, xt_l, pieces, const, ps, **options)
                    use(norm, xt_h, xt_l, *parts)
                else:
                    layer_norm_block(nc, ctx, f"{tag}n", x, xt_h, xt_l, pieces, b_credited, const, ps, **options)
                    use(xt_h, xt_l, *parts)

        def stats_of(tag):
            return sb(f"{tag}_stats", [P, NT, 6]), ctx.enter_context(nc.semaphore(f"{tag}_stats_done"))

        f1_stats, b_stats = stats_of("f1"), stats_of("b")
        a_credited = {n: ctx.enter_context(nc.semaphore(f"ra_{n}")) for n in ROTARY_CREDITED}
        b_credited = {n: ctx.enter_context(nc.semaphore(f"ab_{n}")) for n in ALIBI_CREDITED}

        def ffn(tag, stats=None, next_stats=None, out=None):
            with_xt(tag, [ins["wf"], ins["wb"]], lambda norm, h, l, w_h, w_l, wb_h, wb_l: ffn_block(
                nc, ctx, tag, norm, x, h, l, w_h, w_l, wb_h, wb_l, const, ps, ins["bf"], next_stats, out), stats=stats)

        with ExitStack() as rotary:
            v_all = rotary.enter_context(nc.sbuf_tensor("v_all", [P, NT, C], F32))

            def start(first_norm, h, l, w_h, w_l):
                with nc.Block() as block:
                    @block.sync
                    def _(sp):
                        for name in ("ident", "rel", "trig", "slopes", "iota"):
                            sp.dma_start(const[name][:], ins[name]).then_inc(loaded, 16)
                        sp.dma_start(w_norm2[:, :, :], ins["w_norm"].partition_broadcast(P)).then_inc(loaded, 16)
                        for i in range(NT):
                            sp.dma_start(x[:, i, :], ins["x"][i * P:(i + 1) * P, :]).then_inc(x_in[i * len(x_in) // NT], 16)
                        first_norm.load_weights(sp)
                        sp.wait_ge(loaded, 16 * 6)

                    @block.vector
                    def _(dve):
                        dve.memset(const["neg_half"][:, :], -0.5)
                        dve.wait_ge(loaded, 16 * 6)
                        dve.tensor_copy(const["ident_bf"][:, :], const["ident"][:, :])
                        dve.scalar_tensor_tensor(const["w_norm"][:, :], w_norm2[:, 0, :], DB ** -0.5, w_norm2[:, 1, :],
                                                 ALU.mult, ALU.mult).then_inc(made, 1)
                        dve.wait_ge(made, 1)

                rotary_projection_block(nc, ctx, first_norm, h, l, w_h, w_l, v_all, a_credited, const, ps,
                                        parts_dram, x_in)

            with_xt("a", [ins["wa"]], start, banks=(6, 7, 5), apart=True)
            o_all = rotary.enter_context(nc.sbuf_tensor("o_all", [P, NT, C], F32))
            wo_h = rotary.enter_context(nc.sbuf_tensor("wao_h", [P, KC, C], F32R))
            wo_l = rotary.enter_context(nc.sbuf_tensor("wao_l", [P, KC, C], F32R))
            rotary_attention_block(nc, ctx, v_all, o_all, wo_h, wo_l, a_credited, const, ps, parts_dram, ins["wao"])
            rotary_output_block(nc, ctx, x, o_all, wo_h, wo_l, f1_stats, const, ps)
        ffn("f1", f1_stats, b_stats)
        with_xt("b", [ins["wqkv"][0]], lambda h, l, w_h, w_l: alibi_attention_block(
            nc, ctx, x, h, l, w_h, w_l, b_credited, const, ps, ins["wqkv"], ins["wbo"]), merged=False, stats=b_stats)
        ffn("f2", out=out_dram)



def tables():
    p = np.arange(P, dtype=np.float32)[:, None]
    rel = np.arange(T, dtype=np.float32)[None, :] - np.float32(SLIDE) - p
    rel = np.where(rel > 0, np.float32(NEG), rel).astype(np.float32)
    theta = (np.arange(NT, dtype=np.float32)[None, :] * P + p)
    cos, sin = np.cos(theta), np.sin(theta)
    scale = np.float32(DA ** -0.5)
    trig = np.stack([cos, sin, cos * scale, sin * scale], axis=-1).astype(np.float32)
    start = 2.0 ** (-2.0 ** (-(np.log2(HB) - 3)))
    slopes = np.array([start * start ** i for i in range(HB)], dtype=np.float32)
    return {
        "ident": np.eye(P, dtype=np.float32),
        "rel": rel,
        "trig": trig,
        "slopes": np.tile(slopes[None, :], (P, 1)),
        "iota": np.tile(np.arange(NE, dtype=np.float32)[None, :], (P, 1)),
    }


def layouts(i):
    wq = np.asarray(i["L0_attn_b_Wq"]).reshape(KVB, GB * DB, C)
    wk = np.asarray(i["L0_attn_b_Wk"]).reshape(KVB, DB, C)
    wv = np.asarray(i["L0_attn_b_Wv"]).reshape(KVB, DB, C)
    qkv = np.concatenate([wq, wk, wv], axis=1).transpose(0, 2, 1)
    a = [np.asarray(i[f"L0_attn_a_{n}"]) for n in ("wq", "wk", "wv")]
    lora_a = np.asarray(i["L0_ffn_lora_A"]).reshape(ER, C)
    return {
        "x": np.asarray(i["L0_attn_a_x"]).reshape(T, C),
        "wa": np.concatenate([w.T for w in a], axis=1),
        "wao": np.asarray(i["L0_attn_a_wo"]).T,
        "wqkv": qkv,
        "wbo": np.asarray(i["L0_attn_b_Wo"]).T.reshape(KVB, GB * DB, C),
        "w_norm": np.stack([np.asarray(i["L0_attn_b_q_norm_w"]), np.asarray(i["L0_attn_b_k_norm_w"])]),
        "wf": np.concatenate([np.asarray(i["L0_ffn_W_base"]), lora_a, np.asarray(i["L0_ffn_W_router"])], axis=0).T,
        "wb": np.asarray(i["L0_ffn_lora_B"]).transpose(0, 2, 1).reshape(ER, C),
        "bf": np.asarray(i["L0_ffn_b_base"]),
    }


def kernel(**inputs):
    import concourse.bacc as bacc
    from concourse.bass_utils import run_bass_kernel_spmd

    arrays = {n: np.ascontiguousarray(a) for n, a in {**layouts(inputs), **tables()}.items()}
    nc = bacc.Bacc("TRN2", target_bir_lowering=False, num_devices=1)
    ins = {n: nc.dram_tensor(f"in_{n}", a.shape, mybir.dt.from_np(a.dtype), kind="ExternalInput").ap()
           for n, a in arrays.items()}
    out = nc.dram_tensor("out_0_dram", (T, C), F32, kind="ExternalOutput").ap()
    hybrid_layer_kernel(nc, ins, out)
    r = run_bass_kernel_spmd(nc, [{f"in_{n}": a for n, a in arrays.items()}], core_ids=[0])
    return r.results[0]["out_0_dram"].reshape(1, T, C)
```
